# Optimizing a Trainium2 kernel written in Bass

```python
import numpy as np
import jax
import jax.numpy as jnp

def _softmax(x, axis=-1):
    return jax.nn.softmax(x, axis=axis)
def _gelu(x):
    return jax.nn.gelu(x, approximate=True)
def _silu(x):
    return jax.nn.silu(x)
def _sigmoid(x):
    return jax.nn.sigmoid(x)
def _layernorm(x, axis=-1, eps=1e-5):
    m = jnp.mean(x, axis=axis, keepdims=True)
    v = jnp.var(x, axis=axis, keepdims=True)
    return (x - m) / jnp.sqrt(v + eps)
def _scatter_add(tgt, idx, src, axis=0):
    return tgt.at[idx].add(src)
def _segment_sum(src, seg, n):
    return jax.ops.segment_sum(src, seg, n)

kernel_name = 'mk_conv_preact_d1_conv_nchw256_100192'

def setup_inputs(seed: int = 0):
    np.random.seed(seed)
    _w = jnp.asarray
    def _rec_inputs():
        import jax
        import jax.numpy as jnp
        _gk = jax.random.key(seed)
        x = -0.0003482 + 1 * jax.random.normal(jax.random.fold_in(_gk, 1), (8, 256, 96, 96), jnp.float32)
        return x
    x = _rec_inputs()
    def _L0_conv_setup():
        import jax, jax.numpy as jnp
        import numpy as np
        B, C, COUT, K, R, H, W = (8, 256, 256, 3, 4, 96, 96)
        S = K * K
        L = H * W
        MIN_HYP, MAX_HYP = (0.1, 1.0)
        TEMP = 1.0
        EPS = 0.0001
        _offs = [(float(c - K // 2), float(r - K // 2)) for r in range(K) for c in range(K)]
        DX = np.asarray([o[0] for o in _offs], np.float32).reshape(1, 1, S, 1)
        DY = np.asarray([o[1] for o in _offs], np.float32).reshape(1, 1, S, 1)

        def _inv_softplus(v):
            v = max(v, 1e-06)
            return v + np.log(-np.expm1(-v))

        def _geom_bias():
            cat_theta = np.arctan2((3.0 + np.sqrt(5.0)) / 2.0 - 2.0, 1.0)
            theta_init = cat_theta + np.linspace(0.0, np.pi * (R - 1) / R, R)
            raw_base = _inv_softplus(1.0 - 0.0001)
            hyper_init = min(max(MIN_HYP, 0.5 * 0.35), MAX_HYP)
            raw_hyper = _inv_softplus(hyper_init)
            return np.concatenate([theta_init, np.full(R, raw_base), np.full(R, raw_hyper)]).astype(np.float32)

        def _unfold(v):
            pad = K // 2
            vp = jnp.pad(v, ((0, 0), (0, 0), (pad, pad), (pad, pad)))
            pats = jnp.stack([vp[:, :, r:r + H, c:c + W] for r in range(K) for c in range(K)], axis=2)
            return pats.reshape(B, C, S, L)
        key = jax.random.key(seed)
        ks = jax.random.split(key, 6)
        return {'x': jax.random.normal(ks[0], (B, C, H, W), jnp.float32), 'Wv': jax.random.normal(ks[1], (C, C), jnp.float32) / np.sqrt(C), 'Wg': jax.random.normal(ks[2], (R, C), jnp.float32) / np.sqrt(C), 'bg': jnp.zeros((R,), jnp.float32), 'Wgeom': jax.random.normal(ks[3], (3 * R, C), jnp.float32) * (0.02 / np.sqrt(C)), 'bgeom': jnp.asarray(_geom_bias()), 'Wp': jax.random.normal(ks[4], (COUT, R * C), jnp.float32) / np.sqrt(R * C), 'bp': jnp.zeros((COUT,), jnp.float32)}
    _L0_conv_all = _L0_conv_setup()
    _L0_conv_in = {k: v for k, v in _L0_conv_all.items() if k in ('Wv', 'Wg', 'bg', 'Wgeom', 'bgeom', 'Wp', 'bp', )}
    del _L0_conv_all

    return {
        "x": x,
        "L0_conv_Wv": _L0_conv_in["Wv"],
        "L0_conv_Wg": _L0_conv_in["Wg"],
        "L0_conv_bg": _L0_conv_in["bg"],
        "L0_conv_Wgeom": _L0_conv_in["Wgeom"],
        "L0_conv_bgeom": _L0_conv_in["bgeom"],
        "L0_conv_Wp": _L0_conv_in["Wp"],
        "L0_conv_bp": _L0_conv_in["bp"],
    }

def reference(x, L0_conv_Wv, L0_conv_Wg, L0_conv_bg, L0_conv_Wgeom, L0_conv_bgeom, L0_conv_Wp, L0_conv_bp):
    import jax
    import jax.numpy as jnp
    def _L0_conv_ref(x, Wv, Wg, bg, Wgeom, bgeom, Wp, bp):
        import jax, jax.numpy as jnp
        import numpy as np
        B, C, COUT, K, R, H, W = (8, 256, 256, 3, 4, 96, 96)
        S = K * K
        L = H * W
        MIN_HYP, MAX_HYP = (0.1, 1.0)
        TEMP = 1.0
        EPS = 0.0001
        _offs = [(float(c - K // 2), float(r - K // 2)) for r in range(K) for c in range(K)]
        DX = np.asarray([o[0] for o in _offs], np.float32).reshape(1, 1, S, 1)
        DY = np.asarray([o[1] for o in _offs], np.float32).reshape(1, 1, S, 1)

        def _inv_softplus(v):
            v = max(v, 1e-06)
            return v + np.log(-np.expm1(-v))

        def _geom_bias():
            cat_theta = np.arctan2((3.0 + np.sqrt(5.0)) / 2.0 - 2.0, 1.0)
            theta_init = cat_theta + np.linspace(0.0, np.pi * (R - 1) / R, R)
            raw_base = _inv_softplus(1.0 - 0.0001)
            hyper_init = min(max(MIN_HYP, 0.5 * 0.35), MAX_HYP)
            raw_hyper = _inv_softplus(hyper_init)
            return np.concatenate([theta_init, np.full(R, raw_base), np.full(R, raw_hyper)]).astype(np.float32)

        def _unfold(v):
            pad = K // 2
            vp = jnp.pad(v, ((0, 0), (0, 0), (pad, pad), (pad, pad)))
            pats = jnp.stack([vp[:, :, r:r + H, c:c + W] for r in range(K) for c in range(K)], axis=2)
            return pats.reshape(B, C, S, L)
        xf = x.reshape(B, C, L)
        v = jnp.einsum('oc,bcl->bol', Wv, xf).reshape(B, C, H, W)
        patches = _unfold(v)
        m = jax.nn.softmax((jnp.einsum('rc,bcl->brl', Wg, xf) + bg[:, None]) / TEMP, axis=1)
        geom = jnp.einsum('gc,bcl->bgl', Wgeom, xf) + bgeom[:, None]
        theta = geom[:, :R]
        base = jax.nn.softplus(geom[:, R:2 * R]) + EPS
        hyper = jnp.clip(jax.nn.softplus(geom[:, 2 * R:]), MIN_HYP, MAX_HYP)
        cos_t = jnp.cos(theta)[:, :, None, :]
        sin_t = jnp.sin(theta)[:, :, None, :]
        u = cos_t * DX + sin_t * DY
        s = -sin_t * DX + cos_t * DY
        sig_u = (base * jnp.exp(hyper))[:, :, None, :]
        sig_s = (base * jnp.exp(-hyper))[:, :, None, :]
        comp = jnp.exp(-0.5 * ((u / sig_u) ** 2 + (s / sig_s) ** 2))
        w = m[:, :, None, :] * comp
        w = w / (jnp.sum(w, axis=(1, 2), keepdims=True) + 1e-08)
        agg = jnp.einsum('brsl,bcsl->brcl', w, patches)
        out = jnp.einsum('oi,bil->bol', Wp, agg.reshape(B, R * C, L)) + bp[None, :, None]
        return out.reshape(B, COUT, H, W)

    def _gn(v, G=32, eps=1e-5):
        B_, C_, H_, W_ = v.shape
        g = v.reshape(B_, G, C_ // G, H_, W_)
        m = jnp.mean(g, axis=(2, 3, 4), keepdims=True)
        s = jnp.var(g, axis=(2, 3, 4), keepdims=True)
        return ((g - m) / jnp.sqrt(s + eps)).reshape(v.shape)

    def _ln_c(v, eps=1e-6):
        m = jnp.mean(v, axis=1, keepdims=True)
        s = jnp.var(v, axis=1, keepdims=True)
        return (v - m) / jnp.sqrt(s + eps)

    def _ln_t(v, eps=1e-5):
        m = jnp.mean(v, axis=-1, keepdims=True)
        s = jnp.var(v, axis=-1, keepdims=True)
        return (v - m) / jnp.sqrt(s + eps)

    def _to_tokens(v):
        B_, C_, H_, W_ = v.shape
        return v.reshape(B_, C_, H_ * W_).transpose(0, 2, 1)
    def _from_tokens(t, like):
        B_, C_, H_, W_ = like.shape
        return t.transpose(0, 2, 1).reshape(B_, C_, H_, W_)

    x = x + _L0_conv_ref(_gn(x), L0_conv_Wv, L0_conv_Wg, L0_conv_bg, L0_conv_Wgeom, L0_conv_bgeom, L0_conv_Wp, L0_conv_bp)
    return x


_drawn_inputs = setup_inputs


def setup_inputs(seed=0):
    import zlib

    import numpy as np

    out = dict(_drawn_inputs(seed))
    spreads = {'L0_conv_bg': (0.0, 0.8), 'L0_conv_bp': (0.0, 0.1)}
    factors = {'L0_conv_Wgeom': 38.526}
    for name, (base, spread) in spreads.items():
        noise = np.random.default_rng([zlib.crc32(name.encode()), seed]).standard_normal(out[name].shape)
        drawn = base * np.exp(spread * noise) if base else spread * noise
        out[name] = jnp.asarray(drawn.astype(out[name].dtype))
    for name, factor in factors.items():
        out[name] = (out[name] * factor).astype(out[name].dtype)
    return out
```

```python
from contextlib import ExitStack

import numpy as np

import concourse.bass as bass
from concourse import mybir


B, C, H, W = 8, 256, 96, 96
R = 4
GROUP = 8
GN_EPS = 1e-5
SUM_EPS = 1e-8
BASE_EPS = 1e-4
MIN_HYP, MAX_HYP = 0.1, 1.0
P = 128
CH = C // P
SR = 12
STRIPS = B * H // SR
SPI = H // SR
HR = SR + 2
TR, TW = 6, 14
WIN_R, WIN_W = TR + 2, TW + 2
PAIRS = -(-W // TW)
TILES = 2 * PAIRS
WID = [min(TW, W - TW * j) for j in range(PAIRS)]
PADW = TW * (PAIRS - 1) + WIN_W
PIX = SR * W
K3 = 9
KROWS = K3 * R * 2
XS = 128.0
WS = 2.0 ** 15
N16 = 16
CHUNKS = [(0, 2), (2, 4), (4, 7)]
PMM = 24
UNITS = 2 * len(CHUNKS)
PI_PARTS = (3.140625, 9.67502593994140625e-4, 1.509957990978376432e-7)
ROUND = 1.5 * 2.0 ** 23
SIN = [-1 / 6, 1 / 120, -1 / 5040, 1 / 362880, -1 / 39916800, 1 / 6227020800]
COS = [-1 / 2, 1 / 24, -1 / 720, 1 / 40320, -1 / 3628800, 1 / 479001600]
EXT = [
    [(10, 3, 2), (11, 3, 2)],
    [(0, 6, 2), (3, 6, 4), (18, 6, 2)],
    [(2, 5, 2), (17, 5, 2)],
    [(1, 3, 2), (5, 3, 2), (16, 3, 2), (20, 3, 2)],
    [(12, 1, 1)],
]


def p_schedule():
    cost = []
    for u in range(UNITS):
        a, b = CHUNKS[u // 2]
        cost += [sum(WID[a:b]) * SR] * PMM
    total, acc, slots = sum(cost), 0, [[] for _ in range(TILES)]
    for i, c in enumerate(cost):
        slots[min(TILES - 1, acc * TILES // total)].append(i)
        acc += c
    return slots


PSLOTS = p_schedule()
PDONE = [[i // PMM for i in s if i % PMM == PMM - 1] for s in PSLOTS]


def steered_conv(nc, x, wvT, wpT, wgT, gbias, bp, ident, sel, mask, mask12, gavg, flags, out):
    f32, f16, bf16, i32 = mybir.dt.float32, mybir.dt.float16, mybir.dt.bfloat16, mybir.dt.int32
    ALU, ACT, AX = mybir.AluOpType, mybir.ActivationFunctionType, mybir.AxisListType
    MUL, ADD, SUB, MAX, MIN = ALU.mult, ALU.add, ALU.subtract, ALU.max, ALU.min

    xv = x.rearrange("b (h p) (s r) w -> b s r p h w", p=P, r=SR)
    ov = out.rearrange("b (h p) (s r) w -> b s p h (r w)", p=P, r=SR)
    xb = x.rearrange("b (h p) (s r) w -> b s p h (r w)", p=P, r=SR)

    ctx = ExitStack()
    with ctx:
        def sb(name, shape, dt):
            return ctx.enter_context(nc.sbuf_tensor(name, shape, dt))

        def pb(name, shape, dt):
            return ctx.enter_context(nc.psum_tensor(name, shape, dt))

        def sem(name):
            return ctx.enter_context(nc.semaphore(name))

        xs = sb("xs", [P, 2, CH, HR, W], f32)
        stat_in = sb("stat_in", [P, CH, PIX], f32)
        xn32 = sb("xn32", [P, CH, HR, PADW], f32)
        xw = sb("xw", [P, 2, CH, 2, PAIRS, 2, P], f16)
        xc = sb("xc", [P, CH, 2, K3, P], f16)
        res = sb("res", [P, 2, CH, SR, W], f32)
        agg = sb("agg", [P, 2, 2, CH * R, PIX], f16)
        xT = sb("xT", [P, 2, 4 * P], f16)
        band = sb("band", [P, 2, 2, R, SR * TW], f16)
        wT = sb("wT", [KROWS, 2, SR, W], f16)
        proj = sb("proj", [P, 2, CH * R, C], f16)
        idn = sb("idn", [P, P], f16)
        selw = sb("selw", [KROWS, 3, R, 2, P], f16)
        msk = sb("msk", [P, SR * TW], f16)
        msk12 = sb("msk12", [P, SR * WID[-1]], f16)
        gav = sb("gav", [P, P], f32)
        flg = sb("flg", [P, SPI, 2], f32)
        gb = sb("gb", [P, N16], f32)
        bpt = sb("bpt", [P, CH], f32)
        wg32 = sb("wg32", [P, CH, N16], f32)
        wgr = sb("wgr", [P, CH, N16], f32)
        wg3 = sb("wg3", [P, CH, 3, N16], bf16)
        desc = sb("desc", [P, 1], f32)
        pmax = sb("pmax", [P, 2], f32)
        pbits = sb("pbits", [P, 3], i32)
        st6 = sb("st6", [P, CH, 3, 6], f32)
        mv = sb("mv", [P, SPI, CH, 2], f32)
        mvc = sb("mvc", [P, CH, 2], f32)
        gm = sb("gm", [P, CH], f32)
        dev = sb("dev", [P, SPI, CH], f32)
        qv = sb("qv", [P, SPI, CH], f32)
        vr = sb("vr", [P, 4, CH], f32)
        coef = sb("coef", [P, 2, 2, CH], f32)
        cc = sb("cc", [P, 2, CH], f32)
        cf = sb("cf", [P, 2], f32)
        lg = sb("lg", [P, K3, N16], f32)
        mx = sb("mx", [P, K3], f32)
        lm = sb("lm", [P, K3, R], f32)
        az = sb("az", [P, K3, 2 * R], f32)
        sp = sb("sp", [P, K3, 2 * R], f32)
        e4 = sb("e4", [P, K3, R], f32)
        emp = sb("emp", [P, 2, K3, R], f32)
        ab = sb("ab", [P, 4, K3, R], f32)
        th = sb("th", [P, 4, K3, R], f32)
        pol = sb("pol", [P, 2, K3, R], f32)
        uu = sb("uu", [P, K3, 4, R], f32)
        ea = sb("ea", [P, K3, 4, R], f32)
        eb = sb("eb", [P, K3, 4, R], f32)
        zz = sb("zz", [P, 4, K3], f32)
        wf = sb("wf", [P, K3, 5, R], f32)
        w5 = sb("w5", [P, K3, 5, R, 2], f16)
        wext = sb("wext", [P, K3, 25, R * 2], f16)
        wrow = sb("wrow", [P, K3, KROWS], f16)

        psV = pb("psV", [P, 2, 512], f32)
        psA = pb("psA", [P, 2, 512], f32)
        psP = pb("psP", [P, 2, 512], f32)
        psT = pb("psT", [P, 4 * P * 2], f16)
        psG = pb("psG", [P, 512], f32)
        psW = psG[:, :].bitcast(f16)

        tmp = agg[:, 1].rearrange("p a k n -> p (a k n)").bitcast(f32)
        wv_s = tmp[:, 0:512].rearrange("p (a c) -> p a c", a=2)
        wp_s = tmp[:, 512:2560].rearrange("p (q c) -> p q c", q=2 * R)
        p32 = tmp[:, 2560:4608].rearrange("p (k c) -> p k c", k=CH * R)
        ptm = tmp[:, 4608:6656].rearrange("p (k c) -> p k c", k=CH * R)

        consts_in = sem("consts_in")
        x_in = [sem("x_in0"), sem("x_in1")]
        stat_loaded = [sem("stat_loaded0"), sem("stat_loaded1")]
        stored = [sem("stored0"), sem("stored1")]
        init_done = sem("init_done")
        pT_done = sem("pT_done")
        pT_copied = sem("pT_copied")
        pmax_done = sem("pmax_done")
        wready = sem("wready")
        stats_chain = sem("stats_chain")
        mean_ready = sem("mean_ready")
        gsum_done = sem("gsum_done")
        coef_made = sem("coef_made")
        rstd_ready = sem("rstd_ready")
        ln_done = sem("ln_done")
        coef_chain = sem("coef_chain")
        passed = sem("passed")
        normed = sem("normed")
        edged = sem("edged")
        hi_done = sem("hi_done")
        lo_done = sem("lo_done")
        res_ready = sem("res_ready")
        gates_done = sem("gates_done")
        geo = sem("geo")
        act_geo = sem("act_geo")
        ext_made = sem("ext_made")
        ext_done = sem("ext_done")
        w_turned = sem("w_turned")
        w_copied = sem("w_copied")
        tile_turned = sem("tile_turned")
        tile_copied = sem("tile_copied")
        picked = sem("picked")
        banded = sem("banded")
        agg_done = sem("agg_done")
        agg_hi = sem("agg_hi")
        agg_lo = sem("agg_lo")
        proj_done = sem("proj_done")
        out_added = [sem("out_added0"), sem("out_added1")]

        def windows(h, row):
            v = xn32[:, h, TR * row:TR * row + WIN_R]
            step, size = v.ap[-1][0], v.ap[-2][0]
            return bass.AP(v.tensor, v.offset, [list(v.ap[0]), [TW * step, PAIRS], [size, WIN_R], [step, WIN_W]])

        def rows_by_class(h):
            return xn32[:, h, 1:SR + 1, 1:W + 1].rearrange("p (m k) w -> p k m w", k=3)

        def by_class(v):
            return v.rearrange("p k n -> p (k n)").rearrange("p (k m w) -> p k m w", k=3, w=W)

        def hold(eng):
            eng.sem_inc(passed, 1)

        def wait(eng, s, v):
            if isinstance(v, int) and v <= 0:
                return
            eng.wait_ge(s, v)

        GEO, AGEO, COEF, STAT, FIN, WREADY = 48, 7, 2, 9, 11, 14
        GB, GC = 29, 38
        FIRST = 1
        NCONST = 11

        block = ctx.enter_context(nc.Block())

        @block.sync
        def _(sp_):
            def load_x(m, par):
                b = (m & (STRIPS - 1)) // SPI if not isinstance(m, int) else m // SPI
                s, up, down = m & (SPI - 1), (m + SPI - 1) & (SPI - 1), (m + 1) & (SPI - 1)
                sp_.dma_start(xs[:, par, :, 1:SR + 1, :].rearrange("p h r w -> p h (r w)"),
                              at2(xb, b, s)).then_inc(x_in[par], 16)
                for row, t, r in ((0, up, SR - 1), (HR - 1, down, 0)):
                    sp_.dma_start(xs[:, par, :, row, :], at3(xv, b, t, r)).then_inc(x_in[par], 16)

            def at2(v, b, s):
                return v[b, s]

            def at3(v, b, s, r):
                return v[b, s, r]

            def load_stats(k):
                b = (k & (STRIPS - 1)) // SPI if not isinstance(k, int) else k // SPI
                for h in range(CH):
                    wait(sp_, stats_chain, k * STAT - STAT + 3 * h + 3)
                    hold(sp_)
                    sp_.dma_start(stat_in[:, h], at2(xb, b, k & (SPI - 1))[:, h]).then_inc(stat_loaded[h], 16)

            def step(n, par, load, store):
                if load:
                    load_stats(n + 10)
                    wait(sp_, res_ready, n + 1)
                    wait(sp_, normed, 2 * n + 2)
                    hold(sp_)
                    load_x(n + 2, par)
                if store:
                    for oh in range(CH):
                        wait(sp_, out_added[oh], len(CHUNKS) * n + FIRST)
                    hold(sp_)
                    b = (n - 1) // SPI
                    sp_.dma_start(at2(ov, b, (n - 1) & (SPI - 1)),
                                  res[:, 1 - par].rearrange("p h r w -> p h (r w)")).then_inc(stored[1 - par], 16)

            load_stats(0)
            for dst, src in (
                (wv_s, wvT.rearrange("(a p) c -> p a c", p=P)),
                (wp_s, wpT.rearrange("(q p) c -> p q c", p=P)),
                (wg32[:], wgT.rearrange("(h p) g -> p h g", p=P)),
                (idn[:], ident), (selw[:], sel), (msk[:], mask), (msk12[:], mask12),
                (gav[:], gavg), (flg[:], flags), (gb[:], gbias),
                (bpt[:], bp),
            ):
                sp_.dma_start(dst, src).then_inc(consts_in, 16)
            for k in range(1, 10):
                load_stats(k)
                if k == 7:
                    load_x(0, 0)
                    load_x(1, 1)
            step(0, 0, True, False)
            with sp_.Fori(0, (STRIPS - 2) // 2, 1) as d:
                step(d * 2 + 1, 1, True, True)
                step(d * 2 + 2, 0, True, True)
            step(STRIPS - 1, 1, False, True)
            step(STRIPS, 0, False, True)
            for par in range(2):
                sp_.wait_ge(stored[par], 16 * STRIPS // 2 + 16)

        @block.gpsimd
        def _(pool):
            def prep(m, par):
                wait(pool, normed, 2 * m + 2)
                nc.gpsimd.tensor_tensor(
                    xn32[:, :, 0:HR:HR - 1, 1:W + 1], xn32[:, :, 0:HR:HR - 1, 1:W + 1],
                    cf[:, :].unsqueeze(1).unsqueeze(3).broadcast_to([P, CH, 2, W]), MUL).then_inc(edged, 1)
                for h in range(CH):
                    wait(pool, hi_done, 2 * m + h + 1)
                    nc.gpsimd.tensor_tensor(by_class(xc[:, h, 1]), rows_by_class(h), by_class(xc[:, h, 0]), SUB)
                    for row in range(2):
                        i = nc.gpsimd.tensor_tensor(xw[:, par, h, 1, :, row], windows(h, row), xw[:, par, h, 0, :, row], SUB)
                    i.then_inc(lo_done, 1)

            def residual(n, par):
                wait(pool, stored[par], 16 * (n // 2) + 16 if isinstance(n, int) else (n - par) * 8 + 16)
                hold(pool)
                for h in range(CH):
                    i = nc.gpsimd.tensor_scalar(res[:, par, h], xs[:, par, h, 1:SR + 1], 1.0, bpt[:, h:h + 1], MUL, ADD)
                i.then_inc(res_ready, 1)

            def extend(m):
                wait(pool, geo, GEO * m + GEO)
                wait(pool, w_turned, 2 * m)
                hold(pool)
                for kind, runs in enumerate(EXT):
                    for a, b, n in runs:
                        dst = wext[:, :, a:a + (n - 1) * b + 1:b, :]
                        src = w5[:, :, kind].rearrange("p k r t -> p k (r t)").unsqueeze(2)
                        i = nc.gpsimd.tensor_copy(dst, src.broadcast_to([P, K3, n, 2 * R]))
                i.then_inc(ext_made, 1)
                pool.wait_ge(ext_made, m + 1)
                hold(pool)
                n8, n40, n200 = 2 * R, 5 * 2 * R, 25 * 2 * R
                for ky in range(3):
                    v = wext[:]
                    src = bass.AP(v.tensor, v.offset + 3 * ky * n200 + (2 - ky) * n40 + 2 * n8,
                                  [list(v.ap[0]), [n200 - n8, 3], [n40, 3], [1, 3 * n8]])
                    dst = wrow[:, 3 * ky:3 * ky + 3].rearrange("p k (a n) -> p k a n", a=3)
                    i = nc.gpsimd.tensor_copy(dst, src)
                i.then_inc(ext_done, 1)

            for par in range(2):
                pool.sem_inc(stored[par], 16)
            nc.gpsimd.memset(xn32[:].rearrange("p h r w -> p (h r w)"), 0.0).then_inc(init_done, 1)
            pool.wait_ge(consts_in, 16 * NCONST)
            pool.wait_ge(wready, 6)
            nc.gpsimd.partition_all_reduce(pmax[:, 1:2], pmax[:, 0:1], P, bass.bass_isa.ReduceOp.max).then_inc(pmax_done, 1)
            prep(0, 0)
            extend(0)

            def step(n, par, more):
                if more:
                    prep(n + 1, 1 - par)
                residual(n, par)
                if more:
                    extend(n + 1)

            step(0, 0, True)
            with pool.Fori(0, (STRIPS - 2) // 2, 1) as d:
                step(d * 2 + 1, 1, True)
                step(d * 2 + 2, 0, True)
            step(STRIPS - 1, 1, False)

        @block.scalar
        def _(act):
            def normalise(m, par):
                wait(act, x_in[par], 48 * (m // 2) + 48 if isinstance(m, int) else (m - par) * 24 + 48)
                wait(act, coef_chain, COEF * m + COEF)
                wait(act, lo_done, 2 * m)
                for h in range(CH):
                    nc.scalar.activation(xn32[:, h, :, 1:W + 1], xs[:, par, h], ACT.Identity, bias=cc[:, 1, h:h + 1],
                                         scale=cc[:, 0, h:h + 1]).then_inc(normed, 1)

            def round_hi(m, par):
                wait(act, edged, m + 1)
                wait(act, gates_done, m)
                wait(act, tile_turned, TILES * (m - 1))
                for h in range(CH):
                    nc.scalar.activation(by_class(xc[:, h, 0]), rows_by_class(h), ACT.Copy)
                    for row in range(2):
                        i = nc.scalar.activation(xw[:, par, h, 0, :, row], windows(h, row), ACT.Copy)
                    i.then_inc(hi_done, 1)

            def geo_a(m):
                wait(act, geo, GEO * m + 4)
                nc.scalar.activation(e4[:], lm[:], ACT.Exp).then_inc(act_geo, 1)
                nc.scalar.activation(az[:], lg[:, :, 8:16], ACT.Abs).then_inc(act_geo, 1)
                act.wait_ge(act_geo, m * AGEO + 2)
                nc.scalar.activation(az[:], az[:], ACT.Exp, scale=-1.0).then_inc(act_geo, 1)
                act.wait_ge(act_geo, m * AGEO + 3)
                nc.scalar.activation(az[:], az[:], ACT.Ln, bias=1.0).then_inc(act_geo, 1)

            def geo_b(m, need):
                wait(act, geo, GEO * m + need)
                nc.scalar.activation(emp[:, 0], sp[:, :, R:2 * R], ACT.Exp, scale=-2.0).then_inc(act_geo, 1)
                nc.scalar.activation(emp[:, 1], sp[:, :, R:2 * R], ACT.Exp, scale=2.0).then_inc(act_geo, 1)

            def geo_c(m, need):
                wait(act, geo, GEO * m + need)
                nc.scalar.activation(ea[:], ea[:], ACT.Exp).then_inc(act_geo, 1)

            def w_copy(m, par, ky, batch):
                wait(act, w_turned, 2 * m + batch + 1)
                wait(act, picked, TILES * (m - 1))
                off = (ky % 2) * 3 * P
                src = psW[0:KROWS, off:off + 3 * P].rearrange("k (c r w) -> k c r w", c=3, r=SR // 3)
                dst = wT[:, par, ky:SR:3, :].rearrange("k r (w c) -> k c r w", c=3)
                nc.scalar.activation(dst, src, ACT.Copy).then_inc(w_copied, 1)

            def rstd(f):
                wait(act, mean_ready, f * FIN - FIN + 6)
                nc.scalar.activation(vr[:, 1], vr[:, 0], ACT.Ln).then_inc(ln_done, 1)
                act.wait_ge(ln_done, f)
                nc.scalar.activation(vr[:, 2], vr[:, 1], ACT.Exp, scale=-0.5).then_inc(rstd_ready, 1)

            def tile_copy(g, slot):
                wait(act, tile_turned, g + 1)
                wait(act, agg_done, 2 * (g - 1))
                nc.scalar.activation(xT[:, slot], psT[:, 0:4 * P], ACT.Copy).then_inc(tile_copied, 1)

            def agg_round(n, par, t):
                j, row = t // 2, t % 2
                w = WID[j]
                off = SR * TW * j + row * TR * w
                for h in range(CH):
                    wait(act, agg_done, n * (2 * TILES) + 2 * t + h + 1)
                    nc.scalar.activation(agg[:, par, 0, R * h:R * h + R, off:off + TR * w],
                                         psA[:, h, 0:R * TR * w].rearrange("p (r n) -> p r n", r=R),
                                         ACT.Copy, scale=1.0 / WS).then_inc(agg_hi, 1)

            nc.scalar.preload_act_table_set("natural_log_exp_and_others")
            for k in range(CH * R):
                act.wait_ge(pT_done, k + 1)
                nc.scalar.activation(p32[:, k], psA[:, k % 2, 0:C], ACT.Copy).then_inc(pT_copied, 1)
            rstd(1)
            act.wait_ge(init_done, 1)
            normalise(0, 0)
            round_hi(0, 0)
            geo_a(0)
            geo_b(0, GB)
            geo_c(0, GC)
            w_copy(0, 0, 0, 0)
            w_copy(0, 0, 1, 0)
            w_copy(0, 0, 2, 1)
            tile_copy(0, 0)

            def step(n, par, more, f=None):
                wait(act, proj_done, n * UNITS - UNITS + FIRST)
                for t in range(TILES):
                    agg_round(n, par, t)
                    if more and t == 0:
                        normalise(n + 1, 1 - par)
                    if more and t == 1:
                        round_hi(n + 1, 1 - par)
                    if more and t == 6:
                        geo_a(n + 1)
                    if more and t == 7:
                        geo_b(n + 1, GB)
                    if more and t == 8:
                        geo_c(n + 1, GC)
                    if more and t == 10 and f is not None:
                        rstd(f)
                    if more and t == 11:
                        w_copy(n + 1, 1 - par, 0, 0)
                        w_copy(n + 1, 1 - par, 1, 0)
                    if more and t == 12:
                        w_copy(n + 1, 1 - par, 2, 1)
                    if more or t < TILES - 1:
                        tile_copy(n * TILES + t + 1, (t + 1) % 2)

            step(0, 0, True, 2)
            with act.Fori(0, (STRIPS - 2) // 2, 1) as d:
                step(d * 2 + 1, 1, True)
                step(d * 2 + 2, 0, True, d + 3)
            step(STRIPS - 1, 1, False)

        @block.vector
        def _(dve):
            class Chain:

                def __init__(self, s, base):
                    self.s, self.base, self.n = s, base, 0

                def link(self, ins, hold=True):
                    self.n += 1
                    ins.then_inc(self.s, 1)
                    if hold:
                        dve.wait_ge(self.s, self.base + self.n)

            def tt(o, a, b, op):
                return nc.vector.tensor_tensor(o, a, b, op)

            def ts(o, a, s1, s2, o1, o2):
                return nc.vector.tensor_scalar(o, a, s1, s2, o1, o2)

            def stt(o, a, s, b, o1, o2):
                return nc.vector.scalar_tensor_tensor(o, a, s, b, o1, o2)

            def statistics(k):
                ch = Chain(stats_chain, k * STAT)
                for h in range(CH):
                    wait(dve, stat_loaded[h], k * 16 + 16)
                    for c in range(3):
                        ch.link(nc.vector.bn_stats(st6[:, h, c], stat_in[:, h, c * 384:(c + 1) * 384]), h * 3 + c == 5)
                hold(dve)
                for h in range(CH):
                    ch.link(nc.vector.bn_aggr(mvc[:, h], st6[:, h].rearrange("p c s -> p (c s)")), h == 1)
                ch.link(nc.vector.tensor_copy(mv[:, k & (SPI - 1)], mvc[:]))
                assert ch.n == STAT

            def group_mean(f):
                ch = Chain(mean_ready, f * FIN - FIN)
                dve.wait_ge(gsum_done, f * 2 - 1)
                ch.link(nc.vector.tensor_reduce(gm[:], psG[:, 0:SPI * CH].rearrange("p (k h) -> p h k", h=CH), AX.X, ADD))
                ch.link(tt(dev[:], mv[:, :, :, 0], gm[:].unsqueeze(1).broadcast_to([P, SPI, CH]), SUB))
                ch.link(tt(dev[:], dev[:], dev[:], MUL))
                ch.link(tt(qv[:], dev[:], mv[:, :, :, 1], ADD))

            def group_variance(f):
                ch = Chain(mean_ready, f * FIN - FIN)
                ch.n = 4
                dve.wait_ge(gsum_done, f * 2)
                ch.link(nc.vector.tensor_reduce(vr[:, 3], psG[:, 0:SPI * CH].rearrange("p (k h) -> p h k", h=CH), AX.X, ADD))
                i = ts(vr[:, 0], vr[:, 3], GN_EPS, None, ADD, ALU.bypass)
                ch.link(i)

            def coefficients(f, k):
                ch = Chain(mean_ready, f * FIN - FIN)
                ch.n = 6
                dve.wait_ge(rstd_ready, f)
                slot = (k // SPI) & 1
                ch.link(tt(vr[:, 3], vr[:, 0], vr[:, 2], MUL))
                ch.link(tt(vr[:, 3], vr[:, 3], vr[:, 2], MUL))
                ch.link(ts(vr[:, 3], vr[:, 3], -0.5, 1.5, MUL, ADD))
                ch.link(stt(vr[:, 3], vr[:, 2], XS, vr[:, 3], MUL, MUL))
                ch.link(nc.vector.tensor_copy(coef[:, slot, 0], vr[:, 3]), False)
                stt(coef[:, slot, 1], gm[:], -1.0, vr[:, 3], MUL, MUL).then_inc(coef_made, 1)
                dve.wait_ge(coef_made, f)
                assert ch.n == FIN

            def strip_coefficients(m):
                wait(dve, edged, m)
                slot = ((m // SPI) & 1)
                nc.vector.tensor_copy(cc[:], coef[:, slot]).then_inc(coef_chain, 1)
                nc.vector.tensor_copy(cf[:], flg[:, m & (SPI - 1)]).then_inc(coef_chain, 1)

            def b16(a):
                return a.unsqueeze(2).broadcast_to([P, K3, 4, R])

            def geometry_a(m):
                ch = Chain(geo, m * GEO)
                dve.wait_ge(gates_done, m + 1)
                ch.link(nc.vector.tensor_reduce(lg[:], psG[:, 0:K3 * 48].rearrange("p (k t c) -> p k c t", k=K3, t=3), AX.X, ADD))
                ch.link(stt(lg[:], lg[:], 1.0 / XS, gb[:].unsqueeze(1).broadcast_to([P, K3, N16]), MUL, ADD))
                ch.link(nc.vector.tensor_reduce(mx[:], lg[:, :, 0:R], AX.X, MAX))
                ch.link(tt(lm[:], lg[:, :, 0:R], mx[:].unsqueeze(2).broadcast_to([P, K3, R]), SUB))
                r, k = th[:, 0], th[:, 1]
                ch.link(ts(k, lg[:, :, R:2 * R], 1.0 / np.pi, ROUND, MUL, ADD))
                ch.link(ts(k, k, ROUND, None, SUB, ALU.bypass))
                ch.link(stt(r, k, -PI_PARTS[0], lg[:, :, R:2 * R], MUL, ADD))
                ch.link(stt(r, k, -PI_PARTS[1], r, MUL, ADD))
                ch.link(stt(r, k, -PI_PARTS[2], r, MUL, ADD))
                r2, s, c = th[:, 2], pol[:, 0], pol[:, 1]
                ch.link(tt(r2, r, r, MUL))
                nc_ = len(COS)
                ch.link(ts(s, r2, SIN[-1], None, MUL, ALU.bypass), False)
                ch.link(ts(c, r2, COS[-1], None, MUL, ALU.bypass))
                for q in range(nc_ - 2, -1, -1):
                    ch.link(stt(s, s, SIN[q], r2, ADD, MUL), False)
                    ch.link(stt(c, c, COS[q], r2, ADD, MUL))
                ch.link(stt(uu[:, :, 2], s, 1.0, r, ADD, MUL), False)
                ch.link(ts(uu[:, :, 0], c, 1.0, None, ADD, ALU.bypass))
                ch.link(tt(uu[:, :, 1], uu[:, :, 0], uu[:, :, 2], ADD), False)
                ch.link(tt(uu[:, :, 3], uu[:, :, 0], uu[:, :, 2], SUB))
                ch.link(tt(uu[:], uu[:], uu[:], MUL))
                return ch

            def geometry_b(m, ch):
                dve.wait_ge(act_geo, m * AGEO + 4)
                ch.link(stt(sp[:], lg[:, :, 8:16], 0.0, az[:], MAX, ADD))
                ch.link(ts(sp[:, :, R:2 * R], sp[:, :, R:2 * R], MIN_HYP, MAX_HYP, MAX, MIN))
                gbn = ch.n
                ch.link(ts(ab[:, 2], sp[:, :, 0:R], BASE_EPS, None, ADD, ALU.bypass))
                ch.link(tt(ab[:, 2], ab[:, 2], ab[:, 2], MUL))
                ch.link(nc.vector.reciprocal(ab[:, 2], ab[:, 2]))
                return gbn

            def geometry_c(m, ch):
                dve.wait_ge(act_geo, m * AGEO + 6)
                ch.link(stt(ab[:, 0], emp[:, 0], -0.5, ab[:, 2], MUL, MUL), False)
                ch.link(stt(ab[:, 1], emp[:, 1], -0.5, ab[:, 2], MUL, MUL))
                ch.link(tt(ea[:], uu[:], b16(ab[:, 0]), MUL), False)
                bb = ab[:, 1].unsqueeze(2).broadcast_to([P, K3, 2, R])
                ch.link(tt(eb[:, :, 0:2], uu[:, :, 2:4], bb, MUL), False)
                ch.link(tt(eb[:, :, 2:4], uu[:, :, 0:2], bb, MUL))
                ch.link(tt(ea[:], ea[:], eb[:], ADD))
                return ch.n

            def geometry_d(m, ch):
                dve.wait_ge(act_geo, m * AGEO + 7)
                ch.link(tt(eb[:], ea[:], b16(e4[:]), MUL), False)
                ch.link(nc.vector.tensor_reduce(zz[:, 1], e4[:], AX.X, ADD))
                ch.link(nc.vector.tensor_reduce(zz[:, 0], eb[:].rearrange("p k j r -> p k (j r)"), AX.X, ADD))
                ch.link(stt(zz[:, 0], zz[:, 0], 2.0, zz[:, 1], MUL, ADD))
                ch.link(stt(zz[:, 0], zz[:, 1], SUM_EPS, zz[:, 0], MUL, ADD))
                ch.link(nc.vector.reciprocal(zz[:, 2], zz[:, 0]))
                rz = zz[:, 2].unsqueeze(2)
                ch.link(stt(wf[:, :, 0:4].rearrange("p k j r -> p k (j r)"), eb[:].rearrange("p k j r -> p k (j r)"), WS,
                            rz.broadcast_to([P, K3, 4 * R]), MUL, MUL), False)
                ch.link(stt(wf[:, :, 4], e4[:], WS, rz.broadcast_to([P, K3, R]), MUL, MUL))
                wait(dve, ext_done, m)
                f = wf[:].rearrange("p k j r -> p k (j r)")
                hi = w5[:, :, :, :, 0].rearrange("p k j r -> p k (j r)")
                lo = w5[:, :, :, :, 1].rearrange("p k j r -> p k (j r)")
                ch.link(nc.vector.tensor_copy(hi, f))
                ch.link(tt(lo, f, hi, SUB))
                return ch.n

            def band_mask(n, par, t, v):
                p, part = t // 2, t % 2
                slot, w = (par + p) % 2, WID[p]
                dve.wait_ge(picked, v + 1)
                m = msk[:] if w == TW else msk12[:]
                wait(dve, agg_done, 2 * (v - 2) if part == 0 else 0)
                src = psV[:, :, 0:2 * SR * w].rearrange("p b (r n) -> p b r n", r=2)
                tt(band[:, slot, part, :, 0:SR * w].rearrange("p (b r) n -> p b r n", b=2), src,
                   m.unsqueeze(1).unsqueeze(1).broadcast_to([P, 2, 2, SR * w]), MUL).then_inc(banded, 1)

            def agg_rest(n, par, t):
                j, row = t // 2, t % 2
                w = WID[j]
                off = SR * TW * j + row * TR * w
                for h in range(CH):
                    dve.wait_ge(agg_hi, n * (2 * TILES) + 2 * t + h + 1)
                    stt(agg[:, par, 1, R * h:R * h + R, off:off + TR * w],
                        psA[:, h, 0:R * TR * w].rearrange("p (r n) -> p r n", r=R), 1.0 / WS,
                        agg[:, par, 0, R * h:R * h + R, off:off + TR * w], MUL, SUB).then_inc(agg_lo, 1)

            def add_out(n, par, u):
                oh, (a, b) = u % 2, CHUNKS[u // 2]
                dve.wait_ge(proj_done, n * UNITS + u + 1 + FIRST)
                if u == 0:
                    dve.wait_ge(res_ready, n + 1)
                off = 0
                for j in range(a, b):
                    w = WID[j]
                    o = res[:, par, oh, :, TW * j:TW * j + w]
                    i = stt(o, psP[:, oh, off:off + SR * w].rearrange("p (r n) -> p r n", r=SR), desc[:, 0:1], o, MUL, ADD)
                    off += SR * w
                i.then_inc(out_added[oh], 1)

            def prepare_weights():
                ch = Chain(wready, 0)
                ch.link(nc.vector.tensor_copy(wg3[:, :, 0], wg32[:]))
                ch.link(tt(wgr[:], wg32[:], wg3[:, :, 0], SUB))
                ch.link(nc.vector.tensor_copy(wg3[:, :, 1], wgr[:]))
                ch.link(tt(wgr[:], wgr[:], wg3[:, :, 1], SUB))
                ch.link(nc.vector.tensor_copy(wg3[:, :, 2], wgr[:]))
                dve.wait_ge(pT_copied, CH * R)
                ch.link(nc.vector.tensor_reduce(pmax[:, 0:1], p32.rearrange("p k c -> p (k c)"), AX.X, MAX,
                                                apply_absolute_value=True))
                dve.wait_ge(pmax_done, 1)
                ch.link(ts(pmax[:, 1:2], pmax[:, 1:2], 2.0 ** -100, None, MAX, ALU.bypass))
                ch.link(ts(pbits[:, 0:1], pmax[:, 1:2].bitcast(i32), 0x7F800000, None, ALU.bitwise_and, ALU.bypass))
                ch.link(ts(pbits[:, 1:2], pbits[:, 0:1], -1.0, float(267 << 23), MUL, ADD), False)
                ch.link(ts(pbits[:, 2:3], pbits[:, 0:1], 1.0, float(20 << 23), MUL, SUB))
                ch.link(nc.vector.tensor_copy(desc[:], pbits[:, 2:3].bitcast(f32)), False)
                ch.link(ts(ptm, p32, pbits[:, 1:2].bitcast(f32), None, MUL, ALU.bypass))
                ch.link(nc.vector.tensor_copy(proj[:, 0], ptm))
                ch.link(tt(proj[:, 1], ptm, proj[:, 0], SUB))
                return ch.n

            for oh in range(CH):
                dve.sem_inc(out_added[oh], FIRST)
            for k in range(SPI):
                statistics(k)
            group_mean(1)
            group_variance(1)
            coefficients(1, 0)
            dve.wait_ge(consts_in, 16 * NCONST)
            strip_coefficients(0)
            prepare_weights()
            ch = geometry_a(0)
            geometry_b(0, ch)
            geometry_c(0, ch)
            geometry_d(0, ch)
            assert ch.n == GEO, ch.n
            statistics(SPI)
            band_mask(0, 0, 0, 0)
            band_mask(0, 0, 1, 1)

            def step(n, par, main, more, f=None, before=True):
                ch = None
                if more:
                    strip_coefficients(n + 1)
                for t in range(TILES):
                    if main:
                        agg_rest(n, par, t)
                        if more or t < TILES - 2:
                            last = t >= TILES - 2
                            band_mask(n, (1 - par) if last else par, t + 2 - (TILES if last else 0), n * TILES + t + 2)
                    if before:
                        for u in PDONE[t]:
                            add_out(n - 1, 1 - par, u)
                    if more and t == 2:
                        statistics(n + 9)
                    if more and t == 5:
                        ch = geometry_a(n + 1)
                    if more and t == 6:
                        geometry_b(n + 1, ch)
                    if more and t == 7:
                        geometry_c(n + 1, ch)
                    if more and t == 8:
                        geometry_d(n + 1, ch)
                        assert ch.n == GEO
                    if more and t == 9 and f is not None:
                        group_mean(f)
                    if more and t == 10 and f is not None:
                        group_variance(f)
                    if more and t == 11 and f is not None:
                        coefficients(f, n + 9)

            step(0, 0, True, True, 2, before=False)
            with dve.Fori(0, (STRIPS - 2) // 2, 1) as d:
                step(d * 2 + 1, 1, True, True)
                step(d * 2 + 2, 0, True, True, d + 3)
            step(STRIPS - 1, 1, True, False)
            step(STRIPS, 0, False, False)

        @block.tensor
        def _(pe):
            mm = nc.tensor.matmul

            def turn_tile(n, par, t, g):
                if t == 0:
                    wait(pe, lo_done, 2 * n + 2)
                wait(pe, tile_copied, g)
                for part in range(2):
                    for h in range(CH):
                        q = part * 2 + h
                        i = nc.tensor.transpose(psT[:, q * P:(q + 1) * P],
                                                xw[:, par, h, part, t // 2, t % 2], idn[:])
                i.then_inc(tile_turned, 1)

            def pick(n, par, t, v):
                p, part = t // 2, t % 2
                w, phase = WID[p], (TW * p) % 3
                if t == 0:
                    wait(pe, w_copied, 3 * n + 3)
                wait(pe, banded, v)
                rhs = wT[:, par, :, TW * p:TW * p + w]
                for r in range(R):
                    i = mm(psV[:, r // 2, (r % 2) * SR * w:(r % 2 + 1) * SR * w], selw[:, phase, r, part], rhs,
                           start=True, stop=True)
                i.then_inc(picked, 1)

            def aggregate(n, par, t):
                j, row = t // 2, t % 2
                w = WID[j]
                slot = (par + j) % 2
                wait(pe, tile_copied, n * TILES + t + 1)
                if row == 0:
                    wait(pe, banded, n * TILES + t + 2)
                for h in range(CH):
                    wait(pe, agg_lo, n * (2 * TILES) + 2 * t + h - 1)
                    for q, (xp, bpart) in enumerate(((0, 0), (0, 1), (1, 0))):
                        i = mm(psA[:, h, 0:R * TR * w].rearrange("p (r n) -> p r n", r=R),
                               xT[:, t % 2, (xp * 2 + h) * P:(xp * 2 + h + 1) * P],
                               band[:, slot, bpart, :, row * TR * w:(row + 1) * TR * w], start=q == 0, stop=q == 2)
                    i.then_inc(agg_done, 1)

            def project(n, par, idx):
                u, k = idx // PMM, idx % PMM
                oh, (a, b) = u % 2, CHUNKS[u // 2]
                o0, cols = SR * TW * a, SR * sum(WID[a:b])
                if k == 0:
                    if oh == 0:
                        wait(pe, agg_lo, n * (2 * TILES) + 4 * b)
                    wait(pe, out_added[oh], n * len(CHUNKS) + u // 2 + FIRST)
                kk, q = k // 3, k % 3
                pp, ap = ((0, 0), (0, 1), (1, 0))[q]
                i = mm(psP[:, oh, 0:cols], proj[:, pp, kk, oh * P:(oh + 1) * P], agg[:, par, ap, kk, o0:o0 + cols],
                       start=k == 0, stop=k == PMM - 1)
                if k == PMM - 1:
                    i.then_inc(proj_done, 1)

            def gates(m, par):
                wait(pe, lo_done, 2 * m + 2)
                wait(pe, w_copied, 3 * m)
                for ky in range(3):
                    for kx in range(3):
                        o = psG[:, (ky * 3 + kx) * 48:(ky * 3 + kx + 1) * 48]
                        for q in range(4):
                            part, h = q // 2, q % 2
                            rows = xc[:, h, part].rearrange("p k n -> p (k n)")
                            px = rows[:, ky * 3 * P + kx:(ky + 1) * 3 * P:3]
                            i = mm(o, px, wg3[:, h].rearrange("p t g -> p (t g)"), start=q == 0, stop=q == 3)
                i.then_inc(gates_done, 1)

            def turn_weights(m, batch):
                if batch == 0:
                    wait(pe, ext_done, m + 1)
                else:
                    wait(pe, w_copied, 3 * m + 2)
                for ky in ((0, 1), (2,))[batch]:
                    for kx in range(3):
                        off = (ky % 2) * 3 * P + kx * P
                        i = nc.tensor.transpose(psW[0:KROWS, off:off + P], wrow[:, ky * 3 + kx], idn[:])
                i.then_inc(w_turned, 1)

            def group_sum(f, which, src):
                i = mm(psG[:, 0:SPI * CH], gav[:], src, start=True, stop=True)
                i.then_inc(gsum_done, 1)

            pe.sem_inc(proj_done, FIRST)
            pe.wait_ge(consts_in, 16 * NCONST)
            for k in range(CH * R):
                h, r = k // R, k % R
                wait(pe, pT_copied, k - 1)
                for a in range(2):
                    i = mm(psA[:, k % 2, 0:C], wv_s[:, a, h * P:(h + 1) * P], wp_s[:, 2 * r + a], start=a == 0, stop=a == 1)
                i.then_inc(pT_done, 1)
            means = mv[:, :, :, 0]
            pe.wait_ge(stats_chain, SPI * STAT)
            group_sum(1, 0, means)
            pe.wait_ge(mean_ready, 4)
            group_sum(1, 1, qv[:])
            pe.wait_ge(wready, 5)
            pe.wait_ge(mean_ready, 6)
            gates(0, 0)
            turn_weights(0, 0)
            turn_weights(0, 1)
            turn_tile(0, 0, 0, 0)
            pick(0, 0, 0, 0)
            pick(0, 0, 1, 1)
            pe.wait_ge(wready, WREADY)

            def step(n, par, main, more, f=None, before=True):
                for t in range(TILES):
                    if main:
                        aggregate(n, par, t)
                    if more and t == 4:
                        gates(n + 1, 1 - par)
                    if more and t == 9 and f is not None:
                        wait(pe, stats_chain, (n + 10) * STAT)
                        wait(pe, geo, n * GEO + GEO + 1)
                        group_sum(f, 0, means)
                    if more and t == 10 and f is not None:
                        pe.wait_ge(mean_ready, f * FIN - FIN + 4)
                        group_sum(f, 1, qv[:])
                    if more and t == 11:
                        if f is not None:
                            pe.wait_ge(mean_ready, f * FIN - FIN + 6)
                        turn_weights(n + 1, 0)
                    if before:
                        for idx in PSLOTS[t]:
                            project(n - 1, 1 - par, idx)
                    if more and t == 11:
                        turn_weights(n + 1, 1)
                    if main and (more or t < TILES - 1):
                        last = t == TILES - 1
                        turn_tile(n + 1 if last else n, 1 - par if last else par, 0 if last else t + 1, n * TILES + t + 1)
                    if main and (more or t < TILES - 2):
                        last = t >= TILES - 2
                        pick(n + 1 if last else n, 1 - par if last else par, t + 2 - (TILES if last else 0), n * TILES + t + 2)

            step(0, 0, True, True, 2, before=False)
            with pe.Fori(0, (STRIPS - 2) // 2, 1) as d:
                step(d * 2 + 1, 1, True, True)
                step(d * 2 + 2, 0, True, True, d + 3)
            step(STRIPS - 1, 1, True, False)
            step(STRIPS, 0, False, False)


def shape_tables():
    win = np.arange(P)
    wy, wx = win // WIN_W - 1, win % WIN_W - 1
    sel = np.zeros((K3, R, 2, 3, R, 2, P), np.float16)
    for phase in range(3):
        cls = ((wy % 3) * 3 + (wx + phase) % 3)
        for r in range(R):
            for part in range(2):
                sel[cls, r, part, phase, r, part, win] = 1.0
    sel = sel.reshape(KROWS, 3, R, 2, P)

    def mask(w):
        y, x = np.divmod(np.arange(SR * w), w)
        near = (abs(wy[:, None] - y % TR) <= 1) & (abs(wx[:, None] - x) <= 1)
        return near.astype(np.float16)

    group = np.arange(P) // GROUP
    gavg = (group[:, None] == group).astype(np.float32) / (GROUP * SPI)
    flags = np.ones((P, SPI, 2), np.float32)
    flags[:, 0, 0] = 0.0
    flags[:, SPI - 1, 1] = 0.0
    return {"ident": np.eye(P, dtype=np.float16), "sel": sel, "mask": mask(TW), "mask12": mask(WID[-1]),
            "gavg": gavg, "flags": flags}


def kernel(x, L0_conv_Wv, L0_conv_Wg, L0_conv_bg, L0_conv_Wgeom, L0_conv_bgeom, L0_conv_Wp, L0_conv_bp):
    import concourse.bacc as bacc
    from concourse.bass_utils import run_bass_kernel_spmd

    arrays = {
        "x": np.ascontiguousarray(x),
        "wv": np.ascontiguousarray(L0_conv_Wv),
        "wpT": np.ascontiguousarray(np.asarray(L0_conv_Wp).T),
        "wgT": np.ascontiguousarray(np.concatenate([np.asarray(L0_conv_Wg), np.asarray(L0_conv_Wgeom)]).T),
        "gbias": np.ascontiguousarray(np.broadcast_to(
            np.concatenate([np.asarray(L0_conv_bg), np.asarray(L0_conv_bgeom)]), (P, N16))),
        "bp": np.ascontiguousarray(np.asarray(L0_conv_bp).reshape(CH, P).T),
        **shape_tables(),
    }
    nc = bacc.Bacc("TRN2", target_bir_lowering=False, num_devices=1)
    args = [nc.dram_tensor(f"in_{n}", a.shape, mybir.dt.from_np(a.dtype), kind="ExternalInput").ap()
            for n, a in arrays.items()]
    out = nc.dram_tensor("out", (B, C, H, W), mybir.dt.float32, kind="ExternalOutput").ap()
    steered_conv(nc, *args, out)
    r = run_bass_kernel_spmd(nc, [{f"in_{n}": a for n, a in arrays.items()}], core_ids=[0])
    return r.results[0]["out"]
```

```python
from contextlib import ExitStack

import numpy as np

import concourse.bass as bass
from concourse import mybir


B, C, H, W = 8, 256, 96, 96
R = 4
GROUP = 8
GN_EPS = 1e-5
SUM_EPS = 1e-8
BASE_EPS = 1e-4
MIN_HYP, MAX_HYP = 0.1, 1.0
P = 128
CH = C // P
SR = 12
STRIPS = B * H // SR
SPI = H // SR
HR = SR + 2
TR, TW = 6, 14
WIN_R, WIN_W = TR + 2, TW + 2
PAIRS = -(-W // TW)
TILES = 2 * PAIRS
WID = [min(TW, W - TW * j) for j in range(PAIRS)]
PADW = TW * (PAIRS - 1) + WIN_W
PIX = SR * W
K3 = 9
KROWS = K3 * R * 2
XS = 128.0
WS = 2.0 ** 15
N16 = 16
EARLY = 4
AHEAD = 10
CHUNKS = [(0, 2), (2, 4), (4, 7)]
PMM = 24
UNITS = 2 * len(CHUNKS)
PI_PARTS = (3.140625, 9.67502593994140625e-4, 1.509957990978376432e-7)
ROUND = 1.5 * 2.0 ** 23
SIN = [-1 / 6, 1 / 120, -1 / 5040, 1 / 362880, -1 / 39916800, 1 / 6227020800]
COS = [-1 / 2, 1 / 24, -1 / 720, 1 / 40320, -1 / 3628800, 1 / 479001600]
KINDS = 5
WROWS = 3 * KINDS * R * 2


def p_schedule():
    cost = []
    for u in range(UNITS):
        a, b = CHUNKS[u // 2]
        cost += [sum(WID[a:b]) * SR] * PMM
    total, acc, slots = sum(cost), 0, [[] for _ in range(2 * TILES)]
    for i, c in enumerate(cost):
        slots[min(2 * TILES - 1, acc * 2 * TILES // total)].append(i)
        acc += c
    return slots


PSLOTS = p_schedule()
PDONE = [[i // PMM for i in s if i % PMM == PMM - 1] for s in PSLOTS]


def steered_conv(nc, x, wvT, wpT, wgT, gbias, bp, ident, sel, perm, mask, mask12, gavg, flags, out):
    f32, f16, bf16, i32 = mybir.dt.float32, mybir.dt.float16, mybir.dt.bfloat16, mybir.dt.int32
    ALU, ACT, AX = mybir.AluOpType, mybir.ActivationFunctionType, mybir.AxisListType
    MUL, ADD, SUB, MAX, MIN = ALU.mult, ALU.add, ALU.subtract, ALU.max, ALU.min

    xv = x.rearrange("b (h p) (s r) w -> b s r p h w", p=P, r=SR)
    ov = out.rearrange("b (h p) (s r) w -> b s p h (r w)", p=P, r=SR)
    xb = x.rearrange("b (h p) (s r) w -> b s p h (r w)", p=P, r=SR)

    ctx = ExitStack()
    with ctx:
        def sb(name, shape, dt):
            return ctx.enter_context(nc.sbuf_tensor(name, shape, dt))

        def pb(name, shape, dt):
            return ctx.enter_context(nc.psum_tensor(name, shape, dt))

        def sem(name):
            return ctx.enter_context(nc.semaphore(name))

        xs = sb("xs", [P, 2, CH, HR, W], f32)
        stat_in = sb("stat_in", [P, CH, PIX], f32)
        xn32 = sb("xn32", [P, CH, HR, PADW], f32)
        xw = sb("xw", [P, 2, CH, 2, PAIRS, 2, P], f16)
        xc = sb("xc", [P, CH, 2, K3, P], f16)
        res = sb("res", [P, 2, CH, SR, W], f32)
        agg = sb("agg", [P, 2, 2, CH * R, PIX], f16)
        xT = sb("xT", [P, 2, 4 * P], f16)
        band = sb("band", [P, 2, 2, R, SR * TW], f16)
        wT = sb("wT", [KROWS, 2, SR, W], f16)
        proj = sb("proj", [P, 2, CH * R, C], f16)
        idn = sb("idn", [P, P], f16)
        selw = sb("selw", [KROWS, 3, R, 2, P], f16)
        msk = sb("msk", [P, SR * TW], f16)
        msk12 = sb("msk12", [P, SR * WID[-1]], f16)
        gav = sb("gav", [P, P], f32)
        flg = sb("flg", [P, SPI, 2], f32)
        gb = sb("gb", [P, N16], f32)
        bpt = sb("bpt", [P, CH], f32)
        wg32 = sb("wg32", [P, CH, N16], f32)
        wgr = sb("wgr", [P, CH, N16], f32)
        wg3 = sb("wg3", [P, CH, 3, N16], bf16)
        desc = sb("desc", [P, 1], f32)
        pmax = sb("pmax", [P, 2], f32)
        pbits = sb("pbits", [P, 3], i32)
        st6 = sb("st6", [P, CH, 3, 6], f32)
        mv = sb("mv", [P, SPI, CH, 2], f32)
        mvc = sb("mvc", [P, CH, 2], f32)
        gm = sb("gm", [P, CH], f32)
        dev = sb("dev", [P, SPI, CH], f32)
        qv = sb("qv", [P, SPI, CH], f32)
        vr = sb("vr", [P, 4, CH], f32)
        coef = sb("coef", [P, 2, 2, CH], f32)
        cc = sb("cc", [P, 2, CH], f32)
        cf = sb("cf", [P, 2], f32)
        lg = sb("lg", [P, K3, N16], f32)
        mx = sb("mx", [P, K3], f32)
        lm = sb("lm", [P, K3, R], f32)
        az = sb("az", [P, K3, 2 * R], f32)
        sp = sb("sp", [P, K3, 2 * R], f32)
        e4 = sb("e4", [P, K3, R], f32)
        emp = sb("emp", [P, 2, K3, R], f32)
        ab = sb("ab", [P, 4, K3, R], f32)
        th = sb("th", [P, 4, K3, R], f32)
        pol = sb("pol", [P, 2, K3, R], f32)
        uu = sb("uu", [P, K3, 4, R], f32)
        ea = sb("ea", [P, K3, 4, R], f32)
        eb = sb("eb", [P, K3, 4, R], f32)
        zz = sb("zz", [P, 4, K3], f32)
        wf = sb("wf", [P, K3, 5, R], f32)
        w5 = sb("w5", [P, K3, 5, R, 2], f16)
        wcT = sb("wcT", [WROWS, 3, P], f16)
        prm = sb("prm", [WROWS, K3, KROWS], f16)

        psV = pb("psV", [P, 2, 512], f32)
        psA = pb("psA", [P, 2, 512], f32)
        psP = pb("psP", [P, 2, 512], f32)
        psT = pb("psT", [P, 4 * P * 2], f16)
        psG = pb("psG", [P, 512], f32)
        psG16 = psG[:, :].bitcast(f16)

        tmp = agg[:, 1].rearrange("p a k n -> p (a k n)").bitcast(f32)
        wv_s = tmp[:, 0:512].rearrange("p (a c) -> p a c", a=2)
        wp_s = tmp[:, 512:2560].rearrange("p (q c) -> p q c", q=2 * R)
        p32 = tmp[:, 2560:4608].rearrange("p (k c) -> p k c", k=CH * R)
        ptm = tmp[:, 4608:6656].rearrange("p (k c) -> p k c", k=CH * R)

        early = agg[:, 0].rearrange("p a k n -> p (a k n)").bitcast(f32).rearrange(
            "p (c h n) -> p c h n", c=EARLY, h=CH)

        consts_in = sem("consts_in")
        x_in = [sem("x_in0"), sem("x_in1")]
        stat_loaded = [sem("stat_loaded0"), sem("stat_loaded1")]
        early_in = [sem(f"early_in{c}") for c in range(EARLY)]
        stored = [sem("stored0"), sem("stored1")]
        init_done = sem("init_done")
        pT_done = sem("pT_done")
        pT_copied = sem("pT_copied")
        pmax_done = sem("pmax_done")
        wready = sem("wready")
        stats_chain = sem("stats_chain")
        mean_ready = sem("mean_ready")
        gsum_done = sem("gsum_done")
        coef_made = sem("coef_made")
        rstd_ready = sem("rstd_ready")
        ln_done = sem("ln_done")
        coef_chain = sem("coef_chain")
        passed = sem("passed")
        normed = sem("normed")
        edged = sem("edged")
        xc_hi = sem("xc_hi")
        xc_lo = sem("xc_lo")
        xw_hi = sem("xw_hi")
        xw_lo = sem("xw_lo")
        res_ready = sem("res_ready")
        gates_done = sem("gates_done")
        geo = sem("geo")
        act_geo = sem("act_geo")
        kinds_turned = sem("kinds_turned")
        kinds_copied = sem("kinds_copied")
        w_turned = sem("w_turned")
        w_copied = sem("w_copied")
        tile_turned = sem("tile_turned")
        tile_copied = sem("tile_copied")
        picked = sem("picked")
        banded = sem("banded")
        agg_done = sem("agg_done")
        agg_hi = sem("agg_hi")
        agg_lo = sem("agg_lo")
        proj_done = sem("proj_done")
        out_added = [sem("out_added0"), sem("out_added1")]

        def windows(h, row):
            v = xn32[:, h, TR * row:TR * row + WIN_R]
            step, size = v.ap[-1][0], v.ap[-2][0]
            return bass.AP(v.tensor, v.offset, [list(v.ap[0]), [TW * step, PAIRS], [size, WIN_R], [step, WIN_W]])

        def rows_by_class(h):
            return xn32[:, h, 1:SR + 1, 1:W + 1].rearrange("p (m k) w -> p k m w", k=3)

        def by_class(v):
            return v.rearrange("p k n -> p (k n)").rearrange("p (k m w) -> p k m w", k=3, w=W)

        def hold(eng):
            eng.sem_inc(passed, 1)

        def wait(eng, s, v):
            if isinstance(v, int) and v <= 0:
                return
            eng.wait_ge(s, v)

        GEO, AGEO, COEF, STAT, FIN, WREADY = 48, 7, 2, 9, 11, 14
        G_LOGITS, G_HYPER, G_EXPONENTS = 6, 14, 38
        FIRST = 1
        NCONST = 12

        block = ctx.enter_context(nc.Block())

        @block.sync
        def _(sp_):
            def load_x(m, par):
                b = (m & (STRIPS - 1)) // SPI if not isinstance(m, int) else m // SPI
                s, up, down = m & (SPI - 1), (m + SPI - 1) & (SPI - 1), (m + 1) & (SPI - 1)
                sp_.dma_start(xs[:, par, :, 1:SR + 1, :].rearrange("p h r w -> p h (r w)"),
                              at2(xb, b, s)).then_inc(x_in[par], 16)
                for row, t, r in ((0, up, SR - 1), (HR - 1, down, 0)):
                    sp_.dma_start(xs[:, par, :, row, :], at3(xv, b, t, r)).then_inc(x_in[par], 16)

            def at2(v, b, s):
                return v[b, s]

            def at3(v, b, s, r):
                return v[b, s, r]

            def load_stats(k, h):
                b = (k & (STRIPS - 1)) // SPI if not isinstance(k, int) else k // SPI
                if not isinstance(k, int) or k > SPI:
                    wait(sp_, stats_chain, k * STAT - STAT + 3 * h + 3)
                    hold(sp_)
                sp_.dma_start(stat_in[:, h], at2(xb, b, k & (SPI - 1))[:, h]).then_inc(stat_loaded[h], 16)

            def step(n, par, load, store, stats=True):
                if load and stats:
                    load_stats(n + AHEAD + 1, 0)
                if load:
                    wait(sp_, res_ready, n + 1)
                    wait(sp_, normed, 2 * n + 2)
                    hold(sp_)
                    load_x(n + 2, par)
                if load and stats:
                    load_stats(n + AHEAD + 1, 1)
                if store:
                    b = (n - 1) // SPI
                    dst, src = at2(ov, b, (n - 1) & (SPI - 1)), res[:, 1 - par].rearrange("p h r w -> p h (r w)")
                    if load or stats:
                        for oh in range(CH):
                            wait(sp_, out_added[oh], len(CHUNKS) * n + FIRST)
                        hold(sp_)
                        sp_.dma_start(dst, src).then_inc(stored[1 - par], 16)
                    else:
                        for oh in range(CH):
                            wait(sp_, out_added[oh], len(CHUNKS) * n + FIRST)
                            hold(sp_)
                            sp_.dma_start(dst[:, oh], src[:, oh]).then_inc(stored[1 - par], 16)

            load_x(0, 0)
            load_x(1, 1)
            for dst, src in (
                (wv_s, wvT.rearrange("(a p) c -> p a c", p=P)),
                (wp_s, wpT.rearrange("(q p) c -> p q c", p=P)),
                (wg32[:], wgT.rearrange("(h p) g -> p h g", p=P)),
                (idn[:], ident), (selw[:], sel), (prm[:], perm), (msk[:], mask), (msk12[:], mask12),
                (gav[:], gavg), (flg[:], flags), (gb[:], gbias),
                (bpt[:], bp),
            ):
                sp_.dma_start(dst, src).then_inc(consts_in, 16)
            for k in range(2, 2 + EARLY):
                sp_.dma_start(early[:, k - 2], at2(xb, 0, k)).then_inc(early_in[k - 2], 16)
            load_stats(SPI, 0)
            load_stats(SPI, 1)
            for k in range(2 + EARLY, SPI):
                wait(sp_, stats_chain, (k - EARLY) * STAT + 6)
                hold(sp_)
                sp_.dma_start(early[:, k - 2 - EARLY], at2(xb, 0, k)).then_inc(early_in[k - 2 - EARLY], 16)
            for k in range(SPI + 1, AHEAD + 1):
                load_stats(k, 0)
                load_stats(k, 1)
            step(0, 0, True, False)
            with sp_.Fori(0, (STRIPS - 4) // 2, 1) as d:
                step(d * 2 + 1, 1, True, True)
                step(d * 2 + 2, 0, True, True)
            step(STRIPS - 3, 1, True, True, False)
            step(STRIPS - 2, 0, False, True)
            step(STRIPS - 1, 1, False, True)
            step(STRIPS, 0, False, True, False)
            sp_.wait_ge(stored[0], 16 * STRIPS // 2 + 16)
            sp_.wait_ge(stored[1], 16 * STRIPS // 2 + 32)

        @block.gpsimd
        def _(pool):
            def clear_edges(m):
                wait(pool, normed, 2 * m + 2)
                nc.gpsimd.tensor_tensor(
                    xn32[:, :, 0:HR:HR - 1, 1:W + 1], xn32[:, :, 0:HR:HR - 1, 1:W + 1],
                    cf[:, :].unsqueeze(1).unsqueeze(3).broadcast_to([P, CH, 2, W]), MUL).then_inc(edged, 1)

            def class_lo(m, halves=CH):
                for h in range(halves):
                    wait(pool, xc_hi, 2 * m + h + 1)
                    nc.gpsimd.tensor_tensor(by_class(xc[:, h, 1]), rows_by_class(h), by_class(xc[:, h, 0]),
                                            SUB).then_inc(xc_lo, 1)

            def window_lo(m, par, h):
                for row in range(2):
                    wait(pool, xw_hi, 4 * m + 2 * h + row + 1)
                    i = nc.gpsimd.tensor_tensor(xw[:, par, h, 1, :, row], windows(h, row), xw[:, par, h, 0, :, row], SUB)
                i.then_inc(xw_lo, 1)

            def residual(n, par):
                wait(pool, stored[par], 16 * (n // 2) + 16 if isinstance(n, int) else (n - par) * 8 + 16)
                hold(pool)
                for h in range(CH):
                    i = nc.gpsimd.tensor_scalar(res[:, par, h], xs[:, par, h, 1:SR + 1], 1.0, bpt[:, h:h + 1], MUL, ADD)
                i.then_inc(res_ready, 1)

            for par in range(2):
                pool.sem_inc(stored[par], 16)
            nc.gpsimd.memset(xn32[:].rearrange("p h r w -> p (h r w)"), 0.0).then_inc(init_done, 1)
            pool.wait_ge(consts_in, 16 * NCONST)
            pool.wait_ge(wready, 6)
            nc.gpsimd.partition_all_reduce(pmax[:, 1:2], pmax[:, 0:1], P, bass.bass_isa.ReduceOp.max).then_inc(pmax_done, 1)
            clear_edges(0)
            class_lo(0, 1)
            window_lo(0, 0, 0)
            window_lo(0, 0, 1)
            clear_edges(1)
            class_lo(1)

            def step(n, par, more, ahead):
                residual(n, par)
                if more:
                    for h in range(CH):
                        window_lo(n + 1, 1 - par, h)
                if ahead:
                    clear_edges(n + 2)
                    class_lo(n + 2)

            step(0, 0, True, True)
            with pool.Fori(0, (STRIPS - 4) // 2, 1) as d:
                step(d * 2 + 1, 1, True, True)
                step(d * 2 + 2, 0, True, True)
            step(STRIPS - 3, 1, True, True)
            step(STRIPS - 2, 0, True, False)
            step(STRIPS - 1, 1, False, False)

        @block.scalar
        def _(act):
            def normalise(m, par, h):
                if h == 0:
                    wait(act, x_in[par], 48 * (m // 2) + 48 if isinstance(m, int) else (m - par) * 24 + 48)
                    wait(act, coef_chain, COEF * m + COEF)
                wait(act, xw_lo, 2 * m - 1 + h)
                nc.scalar.activation(xn32[:, h, :, 1:W + 1], xs[:, par, h], ACT.Identity, bias=cc[:, 1, h:h + 1],
                                     scale=cc[:, 0, h:h + 1]).then_inc(normed, 1)

            def class_hi(m, h):
                wait(act, edged, m + 1)
                wait(act, gates_done, m)
                nc.scalar.activation(by_class(xc[:, h, 0]), rows_by_class(h), ACT.Copy).then_inc(xc_hi, 1)

            def window_hi(m, par, h, row):
                wait(act, edged, m + 1)
                wait(act, tile_turned, TILES * (m - 1))
                nc.scalar.activation(xw[:, par, h, 0, :, row], windows(h, row), ACT.Copy).then_inc(xw_hi, 1)

            def geo_a(m):
                wait(act, geo, GEO * m + G_LOGITS)
                nc.scalar.activation(e4[:], lm[:], ACT.Exp).then_inc(act_geo, 1)
                nc.scalar.activation(az[:], lg[:, :, 8:16], ACT.Abs).then_inc(act_geo, 1)
                act.wait_ge(act_geo, m * AGEO + 2)
                nc.scalar.activation(az[:], az[:], ACT.Exp, scale=-1.0).then_inc(act_geo, 1)
                act.wait_ge(act_geo, m * AGEO + 3)
                nc.scalar.activation(az[:], az[:], ACT.Ln, bias=1.0).then_inc(act_geo, 1)

            def geo_b(m):
                wait(act, geo, GEO * m + G_HYPER)
                nc.scalar.activation(emp[:, 0], sp[:, :, R:2 * R], ACT.Exp, scale=-2.0).then_inc(act_geo, 1)
                nc.scalar.activation(emp[:, 1], sp[:, :, R:2 * R], ACT.Exp, scale=2.0).then_inc(act_geo, 1)

            def geo_c(m):
                wait(act, geo, GEO * m + G_EXPONENTS)
                nc.scalar.activation(ea[:], ea[:], ACT.Exp).then_inc(act_geo, 1)

            def kinds_copy(m):
                wait(act, kinds_turned, m + 1)
                nc.scalar.activation(wcT[:].rearrange("k c n -> k (c n)"), psG16[0:WROWS, 0:3 * P],
                                     ACT.Copy).then_inc(kinds_copied, 1)

            def w_copy(m, par, ky):
                wait(act, w_turned, 3 * m + ky + 1)
                wait(act, picked, TILES * (m - 1))
                src = psG[0:KROWS, 0:3 * P].rearrange("k (c r w) -> k c r w", c=3, r=SR // 3)
                dst = wT[:, par, ky:SR:3, :].rearrange("k r (w c) -> k c r w", c=3)
                nc.scalar.activation(dst, src, ACT.Copy).then_inc(w_copied, 1)

            def rstd(f):
                wait(act, mean_ready, f * FIN - FIN + 6)
                nc.scalar.activation(vr[:, 1], vr[:, 0], ACT.Ln).then_inc(ln_done, 1)
                act.wait_ge(ln_done, f)
                nc.scalar.activation(vr[:, 2], vr[:, 1], ACT.Exp, scale=-0.5).then_inc(rstd_ready, 1)

            def tile_copy(g, slot):
                wait(act, tile_turned, g + 1)
                wait(act, agg_done, 2 * (g - 1))
                nc.scalar.activation(xT[:, slot], psT[:, 0:4 * P], ACT.Copy).then_inc(tile_copied, 1)

            def agg_round(n, par, t, h):
                j, row = t // 2, t % 2
                w = WID[j]
                off = SR * TW * j + row * TR * w
                wait(act, agg_done, n * (2 * TILES) + 2 * t + h + 1)
                nc.scalar.activation(agg[:, par, 0, R * h:R * h + R, off:off + TR * w],
                                     psA[:, h, 0:R * TR * w].rearrange("p (r n) -> p r n", r=R),
                                     ACT.Copy, scale=1.0 / WS).then_inc(agg_hi, 1)

            nc.scalar.preload_act_table_set("natural_log_exp_and_others")
            for k in range(CH * R):
                act.wait_ge(pT_done, k + 1)
                nc.scalar.activation(p32[:, k], psA[:, k % 2, 0:C], ACT.Copy).then_inc(pT_copied, 1)
            rstd(1)
            act.wait_ge(init_done, 1)
            for h in range(CH):
                normalise(0, 0, h)
            for h in range(CH):
                class_hi(0, h)
            for h in range(CH):
                for row in range(2):
                    window_hi(0, 0, h, row)
            geo_a(0)
            geo_b(0)
            normalise(1, 1, 0)
            geo_c(0)
            normalise(1, 1, 1)
            tile_copy(0, 0)
            kinds_copy(0)
            for ky in range(3):
                w_copy(0, 0, ky)
            for h in range(CH):
                class_hi(1, h)

            def step(n, par, more, ahead, f=None, first=False):
                wait(act, proj_done, n * UNITS - UNITS + FIRST)
                for t in range(TILES):
                    if more and t == 10:
                        kinds_copy(n + 1)
                    if more and t == 11:
                        w_copy(n + 1, 1 - par, 1)
                    agg_round(n, par, t, 0)
                    if more or t < TILES - 1:
                        tile_copy(n * TILES + t + 1, (t + 1) % 2)
                    if more and t == 10:
                        w_copy(n + 1, 1 - par, 0)
                    if more and t == 11:
                        w_copy(n + 1, 1 - par, 2)
                    agg_round(n, par, t, 1)
                    if more and t == (3 if first else 0):
                        geo_a(n + 1)
                    if more and t in (1, 2, 3, 4):
                        window_hi(n + 1, 1 - par, (t - 1) // 2, (t - 1) % 2)
                    if more and t == 5:
                        geo_b(n + 1)
                    if f is not None and t == 3:
                        rstd(f)
                    if more and t == 7:
                        geo_c(n + 1)
                    if ahead and t in (7, 8):
                        normalise(n + 2, par, t - 7)
                    if ahead and t in (9, 10):
                        class_hi(n + 2, t - 9)

            step(0, 0, True, True, first=True)
            with act.Fori(0, (STRIPS - 4) // 2, 1) as d:
                step(d * 2 + 1, 1, True, True)
                step(d * 2 + 2, 0, True, True, d + 2)
            step(STRIPS - 3, 1, True, True)
            step(STRIPS - 2, 0, True, False)
            step(STRIPS - 1, 1, False, False)

        @block.vector
        def _(dve):
            class Chain:

                def __init__(self, s, base, n=0):
                    self.s, self.base, self.n = s, base, n
                    if n:
                        dve.wait_ge(s, base + n)

                def link(self, ins, hold=True):
                    self.n += 1
                    ins.then_inc(self.s, 1)
                    if hold:
                        dve.wait_ge(self.s, self.base + self.n)

            def tt(o, a, b, op):
                return nc.vector.tensor_tensor(o, a, b, op)

            def ts(o, a, s1, s2, o1, o2):
                return nc.vector.tensor_scalar(o, a, s1, s2, o1, o2)

            def stt(o, a, s, b, o1, o2):
                return nc.vector.scalar_tensor_tensor(o, a, s, b, o1, o2)

            def statistics(k, i):
                h, c = i // 3, i % 3
                if c == 0:
                    wait(dve, stat_loaded[h], k * 16 - (SPI - 1) * 16)
                    wait(dve, stats_chain, k * STAT)
                nc.vector.bn_stats(st6[:, h, c], stat_in[:, h, c * 384:(c + 1) * 384]).then_inc(stats_chain, 1)

            def early_statistics(k):
                if k < 2:
                    dve.wait_ge(x_in[k], 48)
                else:
                    dve.wait_ge(early_in[(k - 2) % EARLY], 16 + 16 * ((k - 2) // EARLY))
                wait(dve, stats_chain, k * STAT)
                for h in range(CH):
                    src = (xs[:, k, h, 1:SR + 1].rearrange("p r w -> p (r w)") if k < 2
                           else early[:, (k - 2) % EARLY, h])
                    for c in range(3):
                        nc.vector.bn_stats(st6[:, h, c], src[:, c * 384:(c + 1) * 384]).then_inc(stats_chain, 1)

            def chunk_moments(k):
                ch = Chain(stats_chain, k * STAT, 6)
                hold(dve)
                for h in range(CH):
                    ch.link(nc.vector.bn_aggr(mvc[:, h], st6[:, h].rearrange("p c s -> p (c s)")), h == 1)
                ch.link(nc.vector.tensor_copy(mv[:, k & (SPI - 1)], mvc[:]))
                assert ch.n == STAT

            def group_mean(f):
                ch = Chain(mean_ready, f * FIN - FIN)
                dve.wait_ge(gsum_done, f * 2 - 1)
                ch.link(nc.vector.tensor_reduce(gm[:], psG[:, 0:SPI * CH].rearrange("p (k h) -> p h k", h=CH), AX.X, ADD))
                ch.link(tt(dev[:], mv[:, :, :, 0], gm[:].unsqueeze(1).broadcast_to([P, SPI, CH]), SUB))
                ch.link(tt(dev[:], dev[:], dev[:], MUL))
                ch.link(tt(qv[:], dev[:], mv[:, :, :, 1], ADD))

            def group_variance(f):
                ch = Chain(mean_ready, f * FIN - FIN, 4)
                dve.wait_ge(gsum_done, f * 2)
                ch.link(nc.vector.tensor_reduce(vr[:, 3], psG[:, 0:SPI * CH].rearrange("p (k h) -> p h k", h=CH), AX.X, ADD))
                i = ts(vr[:, 0], vr[:, 3], GN_EPS, None, ADD, ALU.bypass)
                ch.link(i)

            def coefficients(f, k):
                ch = Chain(mean_ready, f * FIN - FIN, 6)
                dve.wait_ge(rstd_ready, f)
                slot = (k // SPI) & 1
                ch.link(tt(vr[:, 3], vr[:, 0], vr[:, 2], MUL))
                ch.link(tt(vr[:, 3], vr[:, 3], vr[:, 2], MUL))
                ch.link(ts(vr[:, 3], vr[:, 3], -0.5, 1.5, MUL, ADD))
                ch.link(stt(vr[:, 3], vr[:, 2], XS, vr[:, 3], MUL, MUL))
                ch.link(nc.vector.tensor_copy(coef[:, slot, 0], vr[:, 3]), False)
                stt(coef[:, slot, 1], gm[:], -1.0, vr[:, 3], MUL, MUL).then_inc(coef_made, 1)
                dve.wait_ge(coef_made, f)
                assert ch.n == FIN

            def strip_coefficients(m):
                wait(dve, edged, m)
                slot = ((m // SPI) & 1)
                nc.vector.tensor_copy(cc[:], coef[:, slot]).then_inc(coef_chain, 1)
                nc.vector.tensor_copy(cf[:], flg[:, m & (SPI - 1)]).then_inc(coef_chain, 1)

            def b16(a):
                return a.unsqueeze(2).broadcast_to([P, K3, 4, R])

            r_, k_, r2_, s_, c_ = th[:, 0], th[:, 1], th[:, 2], pol[:, 0], pol[:, 1]

            def series(ch, q):
                ch.link(stt(s_, s_, SIN[q], r2_, ADD, MUL), False)
                ch.link(stt(c_, c_, COS[q], r2_, ADD, MUL), False)

            def geometry(m, part):
                if part == 0:
                    ch = Chain(geo, m * GEO)
                    dve.wait_ge(gates_done, m + 1)
                    ch.link(nc.vector.tensor_reduce(
                        lg[:], psG[:, 0:K3 * 48].rearrange("p (k t c) -> p k c t", k=K3, t=3), AX.X, ADD))
                    ch.link(stt(lg[:], lg[:], 1.0 / XS, gb[:].unsqueeze(1).broadcast_to([P, K3, N16]), MUL, ADD), False)
                elif part == 1:
                    ch = Chain(geo, m * GEO, 2)
                    ch.link(nc.vector.tensor_reduce(mx[:], lg[:, :, 0:R], AX.X, MAX), False)
                    ch.link(ts(k_, lg[:, :, R:2 * R], 1.0 / np.pi, ROUND, MUL, ADD))
                    ch.link(tt(lm[:], lg[:, :, 0:R], mx[:].unsqueeze(2).broadcast_to([P, K3, R]), SUB), False)
                    ch.link(ts(k_, k_, ROUND, None, SUB, ALU.bypass), False)
                    assert ch.n == G_LOGITS
                elif part == 2:
                    ch = Chain(geo, m * GEO, 6)
                    ch.link(stt(r_, k_, -PI_PARTS[0], lg[:, :, R:2 * R], MUL, ADD))
                    ch.link(stt(r_, k_, -PI_PARTS[1], r_, MUL, ADD))
                    ch.link(stt(r_, k_, -PI_PARTS[2], r_, MUL, ADD), False)
                elif part == 3:
                    ch = Chain(geo, m * GEO, 9)
                    ch.link(tt(r2_, r_, r_, MUL), False)
                    dve.wait_ge(act_geo, m * AGEO + 4)
                    ch.link(stt(sp[:], lg[:, :, 8:16], 0.0, az[:], MAX, ADD))
                    ch.link(ts(s_, r2_, SIN[-1], None, MUL, ALU.bypass), False)
                    ch.link(ts(c_, r2_, COS[-1], None, MUL, ALU.bypass), False)
                    ch.link(ts(sp[:, :, R:2 * R], sp[:, :, R:2 * R], MIN_HYP, MAX_HYP, MAX, MIN), False)
                    assert ch.n == G_HYPER
                elif part == 4:
                    ch = Chain(geo, m * GEO, 14)
                    series(ch, 4)
                    ch.link(ts(ab[:, 2], sp[:, :, 0:R], BASE_EPS, None, ADD, ALU.bypass))
                    series(ch, 3)
                    ch.link(tt(ab[:, 2], ab[:, 2], ab[:, 2], MUL), False)
                elif part == 5:
                    ch = Chain(geo, m * GEO, 20)
                    series(ch, 2)
                    ch.link(nc.vector.reciprocal(ab[:, 2], ab[:, 2]))
                    series(ch, 1)
                elif part == 6:
                    ch = Chain(geo, m * GEO, 25)
                    series(ch, 0)
                    dve.wait_ge(geo, m * GEO + 27)
                    ch.link(stt(uu[:, :, 2], s_, 1.0, r_, ADD, MUL), False)
                    ch.link(ts(uu[:, :, 0], c_, 1.0, None, ADD, ALU.bypass), False)
                elif part == 7:
                    ch = Chain(geo, m * GEO, 29)
                    ch.link(tt(uu[:, :, 1], uu[:, :, 0], uu[:, :, 2], ADD), False)
                    ch.link(tt(uu[:, :, 3], uu[:, :, 0], uu[:, :, 2], SUB), False)
                    dve.wait_ge(act_geo, m * AGEO + 6)
                    ch.link(stt(ab[:, 0], emp[:, 0], -0.5, ab[:, 2], MUL, MUL), False)
                    ch.link(stt(ab[:, 1], emp[:, 1], -0.5, ab[:, 2], MUL, MUL))
                    ch.link(tt(uu[:], uu[:], uu[:], MUL), False)
                elif part == 8:
                    ch = Chain(geo, m * GEO, 34)
                    ch.link(tt(ea[:], uu[:], b16(ab[:, 0]), MUL), False)
                    bb = ab[:, 1].unsqueeze(2).broadcast_to([P, K3, 2, R])
                    ch.link(tt(eb[:, :, 0:2], uu[:, :, 2:4], bb, MUL), False)
                    ch.link(tt(eb[:, :, 2:4], uu[:, :, 0:2], bb, MUL))
                    ch.link(tt(ea[:], ea[:], eb[:], ADD), False)
                    assert ch.n == G_EXPONENTS
                elif part == 9:
                    ch = Chain(geo, m * GEO, 38)
                    dve.wait_ge(act_geo, m * AGEO + 7)
                    ch.link(tt(eb[:], ea[:], b16(e4[:]), MUL), False)
                    ch.link(nc.vector.tensor_reduce(zz[:, 1], e4[:], AX.X, ADD))
                    ch.link(nc.vector.tensor_reduce(zz[:, 0], eb[:].rearrange("p k j r -> p k (j r)"), AX.X, ADD))
                    ch.link(stt(zz[:, 0], zz[:, 0], 2.0, zz[:, 1], MUL, ADD), False)
                elif part == 10:
                    ch = Chain(geo, m * GEO, 42)
                    ch.link(stt(zz[:, 0], zz[:, 1], SUM_EPS, zz[:, 0], MUL, ADD))
                    ch.link(nc.vector.reciprocal(zz[:, 2], zz[:, 0]))
                    rz = zz[:, 2].unsqueeze(2)
                    ch.link(stt(wf[:, :, 0:4].rearrange("p k j r -> p k (j r)"), eb[:].rearrange("p k j r -> p k (j r)"),
                                WS, rz.broadcast_to([P, K3, 4 * R]), MUL, MUL), False)
                    ch.link(stt(wf[:, :, 4], e4[:], WS, rz.broadcast_to([P, K3, R]), MUL, MUL))
                    wait(dve, kinds_turned, m)
                    f = wf[:].rearrange("p k j r -> p k (j r)")
                    hi = w5[:, :, :, :, 0].rearrange("p k j r -> p k (j r)")
                    lo = w5[:, :, :, :, 1].rearrange("p k j r -> p k (j r)")
                    ch.link(nc.vector.tensor_copy(hi, f))
                    ch.link(tt(lo, f, hi, SUB), False)
                    assert ch.n == GEO

            def band_mask(n, par, t, v):
                p, part = t // 2, t % 2
                slot, w = (par + p) % 2, WID[p]
                dve.wait_ge(picked, v + 1)
                m = msk[:] if w == TW else msk12[:]
                wait(dve, agg_done, 2 * (v - 2) if part == 0 else 0)
                src = psV[:, :, 0:2 * SR * w].rearrange("p b (r n) -> p b r n", r=2)
                tt(band[:, slot, part, :, 0:SR * w].rearrange("p (b r) n -> p b r n", b=2), src,
                   m.unsqueeze(1).unsqueeze(1).broadcast_to([P, 2, 2, SR * w]), MUL).then_inc(banded, 1)

            def agg_rest(n, par, t, h):
                j, row = t // 2, t % 2
                w = WID[j]
                off = SR * TW * j + row * TR * w
                dve.wait_ge(agg_hi, n * (2 * TILES) + 2 * t + h + 1)
                stt(agg[:, par, 1, R * h:R * h + R, off:off + TR * w],
                    psA[:, h, 0:R * TR * w].rearrange("p (r n) -> p r n", r=R), 1.0 / WS,
                    agg[:, par, 0, R * h:R * h + R, off:off + TR * w], MUL, SUB).then_inc(agg_lo, 1)

            def add_out(n, par, u):
                oh, (a, b) = u % 2, CHUNKS[u // 2]
                dve.wait_ge(proj_done, n * UNITS + u + 1 + FIRST)
                if u == 0:
                    dve.wait_ge(res_ready, n + 1)
                off = 0
                for j in range(a, b):
                    w = WID[j]
                    o = res[:, par, oh, :, TW * j:TW * j + w]
                    i = stt(o, psP[:, oh, off:off + SR * w].rearrange("p (r n) -> p r n", r=SR), desc[:, 0:1], o, MUL, ADD)
                    off += SR * w
                i.then_inc(out_added[oh], 1)

            def prepare_gates():
                ch = Chain(wready, 0)
                ch.link(nc.vector.tensor_copy(wg3[:, :, 0], wg32[:]))
                ch.link(tt(wgr[:], wg32[:], wg3[:, :, 0], SUB))
                ch.link(nc.vector.tensor_copy(wg3[:, :, 1], wgr[:]))
                ch.link(tt(wgr[:], wgr[:], wg3[:, :, 1], SUB))
                ch.link(nc.vector.tensor_copy(wg3[:, :, 2], wgr[:]))
                dve.wait_ge(pT_copied, CH * R)
                ch.link(nc.vector.tensor_reduce(pmax[:, 0:1], p32.rearrange("p k c -> p (k c)"), AX.X, MAX,
                                                apply_absolute_value=True), False)

            def prepare_weights():
                ch = Chain(wready, 0, 6)
                dve.wait_ge(pmax_done, 1)
                ch.link(ts(pmax[:, 1:2], pmax[:, 1:2], 2.0 ** -100, None, MAX, ALU.bypass))
                ch.link(ts(pbits[:, 0:1], pmax[:, 1:2].bitcast(i32), 0x7F800000, None, ALU.bitwise_and, ALU.bypass))
                ch.link(ts(pbits[:, 1:2], pbits[:, 0:1], -1.0, float(267 << 23), MUL, ADD), False)
                ch.link(ts(pbits[:, 2:3], pbits[:, 0:1], 1.0, float(20 << 23), MUL, SUB))
                ch.link(nc.vector.tensor_copy(desc[:], pbits[:, 2:3].bitcast(f32)), False)
                ch.link(ts(ptm, p32, pbits[:, 1:2].bitcast(f32), None, MUL, ALU.bypass))
                ch.link(nc.vector.tensor_copy(proj[:, 0], ptm))
                ch.link(tt(proj[:, 1], ptm, proj[:, 0], SUB), False)
                assert ch.n == WREADY

            for oh in range(CH):
                dve.sem_inc(out_added[oh], FIRST)
            for k in range(SPI):
                early_statistics(k)
                chunk_moments(k)
                if k == SPI - 3:
                    dve.wait_ge(consts_in, 16 * NCONST)
                    prepare_gates()
                if k == SPI - 2:
                    prepare_weights()
            group_mean(1)
            group_variance(1)
            coefficients(1, 0)
            strip_coefficients(0)
            dve.wait_ge(xc_hi, 2)
            tt(by_class(xc[:, 1, 1]), rows_by_class(1), by_class(xc[:, 1, 0]), SUB).then_inc(xc_lo, 1)
            strip_coefficients(1)
            for part in range(11):
                geometry(0, part)
            for k in range(SPI, AHEAD):
                for i in range(3 * CH):
                    statistics(k, i)
                chunk_moments(k)
            for i in range(4):
                statistics(AHEAD, i)
            for t in range(2):
                band_mask(0, 0, t, t)

            def step(n, par, main, more, ahead, f=None, before=True, stats=True):
                parts = [(t + 1,) if t <= 9 else () for t in range(TILES)]
                if not before:
                    parts[:8] = [(), (), (), (0, 1), (2, 3), (4, 5), (6, 7), (8,)]

                for t in range(TILES):
                    if main and (more or t < TILES - 2):
                        last = t >= TILES - 2
                        band_mask(n, (1 - par) if last else par, t + 2 - (TILES if last else 0), n * TILES + t + 2)
                    if main:
                        agg_rest(n, par, t, 0)
                    if before:
                        for u in PDONE[2 * t]:
                            add_out(n - 1, 1 - par, u)
                    if more:
                        for part in parts[t]:
                            geometry(n + 1, part)
                    if f is not None:
                        if t == 1:
                            group_mean(f)
                        if t == 3:
                            group_variance(f)
                        if t == 5:
                            coefficients(f, n + SPI + 1)
                    if ahead and t in (0, 3):
                        statistics(n + AHEAD, 4 + t // 3)
                    if ahead and t == 7:
                        chunk_moments(n + AHEAD)
                    if ahead and stats and t in (10, 12):
                        for i in range(2):
                            statistics(n + AHEAD + 1, t - 10 + i)
                    if ahead and t == 6:
                        strip_coefficients(n + 2)
                    if ahead and t == TILES - 1:
                        geometry(n + 2, 0)
                    if main:
                        agg_rest(n, par, t, 1)
                    if before:
                        for u in PDONE[2 * t + 1]:
                            add_out(n - 1, 1 - par, u)

            step(0, 0, True, True, True, before=False)
            with dve.Fori(0, (STRIPS - 4) // 2, 1) as d:
                step(d * 2 + 1, 1, True, True, True)
                step(d * 2 + 2, 0, True, True, True, d + 2)
            step(STRIPS - 3, 1, True, True, True, stats=False)
            step(STRIPS - 2, 0, True, True, False)
            step(STRIPS - 1, 1, True, False, False)
            step(STRIPS, 0, False, False, False)

        @block.tensor
        def _(pe):
            mm = nc.tensor.matmul

            def turn_tile(n, par, t, g):
                if t == 0:
                    wait(pe, xw_lo, 2 * n + 2)
                wait(pe, tile_copied, g)
                for part in range(2):
                    for h in range(CH):
                        q = part * 2 + h
                        i = nc.tensor.transpose(psT[:, q * P:(q + 1) * P],
                                                xw[:, par, h, part, t // 2, t % 2], idn[:])
                i.then_inc(tile_turned, 1)

            def pick(n, par, t, v):
                p, part = t // 2, t % 2
                w, phase = WID[p], (TW * p) % 3
                if t == 0:
                    wait(pe, w_copied, 3 * n + 3)
                wait(pe, banded, v)
                rhs = wT[:, par, :, TW * p:TW * p + w]
                for r in range(R):
                    i = mm(psV[:, r // 2, (r % 2) * SR * w:(r % 2 + 1) * SR * w], selw[:, phase, r, part], rhs,
                           start=True, stop=True)
                i.then_inc(picked, 1)

            def aggregate(n, par, t, h):
                j, row = t // 2, t % 2
                w = WID[j]
                slot = (par + j) % 2
                if h == 0:
                    wait(pe, tile_copied, n * TILES + t + 1)
                    if row == 0:
                        wait(pe, banded, n * TILES + t + 2)
                wait(pe, agg_lo, n * (2 * TILES) + 2 * t + h - 1)
                for q, (xp, bpart) in enumerate(((0, 0), (0, 1), (1, 0))):
                    i = mm(psA[:, h, 0:R * TR * w].rearrange("p (r n) -> p r n", r=R),
                           xT[:, t % 2, (xp * 2 + h) * P:(xp * 2 + h + 1) * P],
                           band[:, slot, bpart, :, row * TR * w:(row + 1) * TR * w], start=q == 0, stop=q == 2)
                i.then_inc(agg_done, 1)

            def project(n, par, idx):
                u, k = idx // PMM, idx % PMM
                oh, (a, b) = u % 2, CHUNKS[u // 2]
                o0, cols = SR * TW * a, SR * sum(WID[a:b])
                if k == 0:
                    if oh == 0:
                        wait(pe, agg_lo, n * (2 * TILES) + 4 * b)
                    wait(pe, out_added[oh], n * len(CHUNKS) + u // 2 + FIRST)
                kk, q = k // 3, k % 3
                pp, ap = ((0, 0), (0, 1), (1, 0))[q]
                i = mm(psP[:, oh, 0:cols], proj[:, pp, kk, oh * P:(oh + 1) * P], agg[:, par, ap, kk, o0:o0 + cols],
                       start=k == 0, stop=k == PMM - 1)
                if k == PMM - 1:
                    i.then_inc(proj_done, 1)

            def gates(m, par):
                wait(pe, xc_lo, 2 * m + 2)
                wait(pe, w_copied, 3 * m)
                for ky in range(3):
                    for kx in range(3):
                        o = psG[:, (ky * 3 + kx) * 48:(ky * 3 + kx + 1) * 48]
                        for q in range(4):
                            part, h = q // 2, q % 2
                            rows = xc[:, h, part].rearrange("p k n -> p (k n)")
                            px = rows[:, ky * 3 * P + kx:(ky + 1) * 3 * P:3]
                            i = mm(o, px, wg3[:, h].rearrange("p t g -> p (t g)"), start=q == 0, stop=q == 3)
                i.then_inc(gates_done, 1)

            def turn_kinds(m):
                wait(pe, geo, GEO * m + GEO)
                for ky in range(3):
                    i = nc.tensor.transpose(psG16[0:WROWS, ky * P:(ky + 1) * P],
                                            w5[:, 3 * ky:3 * ky + 3].rearrange("p k j r t -> p (k j r t)"), idn[:])
                i.then_inc(kinds_turned, 1)

            def turn_weights(m, ky):
                if ky == 0:
                    wait(pe, kinds_copied, m + 1)
                else:
                    wait(pe, w_copied, 3 * m + ky)
                for kx in range(3):
                    i = mm(psG[0:KROWS, kx * P:(kx + 1) * P], prm[:, 3 * ky + kx], wcT[:, ky], start=True, stop=True)
                i.then_inc(w_turned, 1)

            def group_sum(f, which, src):
                i = mm(psG[:, 0:SPI * CH], gav[:], src, start=True, stop=True)
                i.then_inc(gsum_done, 1)

            pe.sem_inc(proj_done, FIRST)
            pe.wait_ge(consts_in, 16 * NCONST)
            for k in range(CH * R):
                h, r = k // R, k % R
                wait(pe, pT_copied, k - 1)
                for a in range(2):
                    i = mm(psA[:, k % 2, 0:C], wv_s[:, a, h * P:(h + 1) * P], wp_s[:, 2 * r + a], start=a == 0, stop=a == 1)
                i.then_inc(pT_done, 1)
            means = mv[:, :, :, 0]
            pe.wait_ge(stats_chain, SPI * STAT)
            group_sum(1, 0, means)
            pe.wait_ge(mean_ready, 4)
            group_sum(1, 1, qv[:])
            pe.wait_ge(wready, 5)
            pe.wait_ge(mean_ready, 6)
            gates(0, 0)
            turn_tile(0, 0, 0, 0)
            turn_kinds(0)
            for ky in range(3):
                turn_weights(0, ky)
            for t in range(3):
                pick(0, 0, t, t)
            pe.wait_ge(wready, WREADY)

            def step(n, par, main, more, ahead, f=None, before=True):
                for t in range(TILES):
                    if main:
                        aggregate(n, par, t, 0)
                    if before:
                        for idx in PSLOTS[2 * t]:
                            project(n - 1, 1 - par, idx)
                    if main and (more or t < TILES - 1):
                        last = t == TILES - 1
                        turn_tile(n + 1 if last else n, 1 - par if last else par, 0 if last else t + 1, n * TILES + t + 1)
                    if more and t == 10:
                        turn_weights(n + 1, 0)
                    if more and t == 11:
                        turn_weights(n + 1, 2)
                    if not before and t == 2:
                        gates(1, 1)
                    if main:
                        aggregate(n, par, t, 1)
                    if before:
                        for idx in PSLOTS[2 * t + 1]:
                            project(n - 1, 1 - par, idx)
                    if f is not None and t == 0:
                        wait(pe, stats_chain, (n + AHEAD) * STAT)
                        wait(pe, geo, n * GEO + GEO + 1)
                        group_sum(f, 0, means)
                    if f is not None and t == 2:
                        pe.wait_ge(mean_ready, f * FIN - FIN + 4)
                        group_sum(f, 1, qv[:])
                    if more and t == 9:
                        if f is not None:
                            pe.wait_ge(mean_ready, f * FIN - FIN + 6)
                        turn_kinds(n + 1)
                    if more and t == 10:
                        turn_weights(n + 1, 1)
                    if ahead and t == 12:
                        gates(n + 2, par)
                    if main and (more or t < TILES - 3):
                        last = t >= TILES - 3
                        pick(n + 1 if last else n, 1 - par if last else par, t + 3 - (TILES if last else 0), n * TILES + t + 3)

            step(0, 0, True, True, True, before=False)
            with pe.Fori(0, (STRIPS - 4) // 2, 1) as d:
                step(d * 2 + 1, 1, True, True, True)
                step(d * 2 + 2, 0, True, True, True, d + 2)
            step(STRIPS - 3, 1, True, True, True)
            step(STRIPS - 2, 0, True, True, False)
            step(STRIPS - 1, 1, True, False, False)
            step(STRIPS, 0, False, False, False)


def shape_tables():
    win = np.arange(P)
    wy, wx = win // WIN_W - 1, win % WIN_W - 1
    sel = np.zeros((K3, R, 2, 3, R, 2, P), np.float16)
    for phase in range(3):
        cls = ((wy % 3) * 3 + (wx + phase) % 3)
        for r in range(R):
            for part in range(2):
                sel[cls, r, part, phase, r, part, win] = 1.0
    sel = sel.reshape(KROWS, 3, R, 2, P)

    kind = {(0, 1): 0, (0, -1): 0, (1, 1): 1, (-1, -1): 1, (1, 0): 2, (-1, 0): 2, (1, -1): 3, (-1, 1): 3, (0, 0): 4}
    perm = np.zeros((3, KINDS, R, 2, K3, K3, R, 2), np.float16)
    for c in range(K3):
        for a in range(K3):
            dy, dx = [(a // 3 - c // 3 + 1) % 3 - 1, (a % 3 - c % 3 + 1) % 3 - 1]
            for r in range(R):
                for part in range(2):
                    perm[c % 3, kind[dy, dx], r, part, c, a, r, part] = 1.0
    perm = perm.reshape(WROWS, K3, KROWS)

    def mask(w):
        y, x = np.divmod(np.arange(SR * w), w)
        near = (abs(wy[:, None] - y % TR) <= 1) & (abs(wx[:, None] - x) <= 1)
        return near.astype(np.float16)

    group = np.arange(P) // GROUP
    gavg = (group[:, None] == group).astype(np.float32) / (GROUP * SPI)
    flags = np.ones((P, SPI, 2), np.float32)
    flags[:, 0, 0] = 0.0
    flags[:, SPI - 1, 1] = 0.0
    return {"ident": np.eye(P, dtype=np.float16), "sel": sel, "perm": perm, "mask": mask(TW), "mask12": mask(WID[-1]),
            "gavg": gavg, "flags": flags}


def kernel(x, L0_conv_Wv, L0_conv_Wg, L0_conv_bg, L0_conv_Wgeom, L0_conv_bgeom, L0_conv_Wp, L0_conv_bp):
    import concourse.bacc as bacc
    from concourse.bass_utils import run_bass_kernel_spmd

    arrays = {
        "x": np.ascontiguousarray(x),
        "wv": np.ascontiguousarray(L0_conv_Wv),
        "wpT": np.ascontiguousarray(np.asarray(L0_conv_Wp).T),
        "wgT": np.ascontiguousarray(np.concatenate([np.asarray(L0_conv_Wg), np.asarray(L0_conv_Wgeom)]).T),
        "gbias": np.ascontiguousarray(np.broadcast_to(
            np.concatenate([np.asarray(L0_conv_bg), np.asarray(L0_conv_bgeom)]), (P, N16))),
        "bp": np.ascontiguousarray(np.asarray(L0_conv_bp).reshape(CH, P).T),
        **shape_tables(),
    }
    nc = bacc.Bacc("TRN2", target_bir_lowering=False, num_devices=1)
    args = [nc.dram_tensor(f"in_{n}", a.shape, mybir.dt.from_np(a.dtype), kind="ExternalInput").ap()
            for n, a in arrays.items()]
    out = nc.dram_tensor("out", (B, C, H, W), mybir.dt.float32, kind="ExternalOutput").ap()
    steered_conv(nc, *args, out)
    r = run_bass_kernel_spmd(nc, [{f"in_{n}": a for n, a in arrays.items()}], core_ids=[0])
    return r.results[0]["out"]
```

```python
from contextlib import ExitStack

import numpy as np

import concourse.bass as bass
from concourse import mybir


B, C, H, W = 8, 256, 96, 96
R = 4
GROUP = 8
GN_EPS = 1e-5
SUM_EPS = 1e-8
BASE_EPS = 1e-4
MIN_HYP, MAX_HYP = 0.1, 1.0
P = 128
CH = C // P
SR = 12
STRIPS = B * H // SR
SPI = H // SR
HR = SR + 2
TR, TW = 6, 14
WIN_R, WIN_W = TR + 2, TW + 2
PAIRS = -(-W // TW)
TILES = 2 * PAIRS
WID = [min(TW, W - TW * j) for j in range(PAIRS)]
PADW = TW * (PAIRS - 1) + WIN_W
PIX = SR * W
K3 = 9
KROWS = K3 * R * 2
XS = 128.0
WS = 2.0 ** 15
N16 = 16
EARLY = 4
AHEAD = 10
CHUNKS = [(0, 2), (2, 4), (4, 7)]
PMM = 24
UNITS = 2 * len(CHUNKS)
PI_PARTS = (3.140625, 9.67502593994140625e-4, 1.509957990978376432e-7)
ROUND = 1.5 * 2.0 ** 23
SIN = [-1 / 6, 1 / 120, -1 / 5040, 1 / 362880, -1 / 39916800, 1 / 6227020800]
COS = [-1 / 2, 1 / 24, -1 / 720, 1 / 40320, -1 / 3628800, 1 / 479001600]
KINDS = 5
WROWS = 3 * KINDS * R * 2


def p_schedule():
    late = 2 * (len(CHUNKS) - 1) * PMM
    order = [(True, i) for i in range(late, UNITS * PMM)] + [(False, i) for i in range(late)]
    cost = [sum(WID[CHUNKS[i // PMM // 2][0]:CHUNKS[i // PMM // 2][1]]) * SR for _, i in order]
    total, acc, slots = sum(cost), 0, [[] for _ in range(2 * TILES)]
    for o, c in zip(order, cost):
        slots[acc * 2 * TILES // total].append(o)
        acc += c
    return slots


PSLOTS = p_schedule()
PDONE = [[(late, i // PMM) for late, i in s if i % PMM == PMM - 1] for s in PSLOTS]


def units(slot, before, main):
    return [(int(late), u) for late, u in slot if (before if late else main)]


def steered_conv(nc, x, wvT, wpT, wgT, gbias, bp, ident, sel, perm, mask, mask12, gavg, flags, out):
    f32, f16, bf16, i32 = mybir.dt.float32, mybir.dt.float16, mybir.dt.bfloat16, mybir.dt.int32
    ALU, ACT, AX = mybir.AluOpType, mybir.ActivationFunctionType, mybir.AxisListType
    MUL, ADD, SUB, MAX, MIN = ALU.mult, ALU.add, ALU.subtract, ALU.max, ALU.min

    xv = x.rearrange("b (h p) (s r) w -> b s r p h w", p=P, r=SR)
    ov = out.rearrange("b (h p) (s r) w -> b s p h (r w)", p=P, r=SR)
    xb = x.rearrange("b (h p) (s r) w -> b s p h (r w)", p=P, r=SR)

    ctx = ExitStack()
    with ctx:
        def sb(name, shape, dt):
            return ctx.enter_context(nc.sbuf_tensor(name, shape, dt))

        def pb(name, shape, dt):
            return ctx.enter_context(nc.psum_tensor(name, shape, dt))

        def sem(name):
            return ctx.enter_context(nc.semaphore(name))

        xs = sb("xs", [P, 2, CH, HR, W], f32)
        stat_in = sb("stat_in", [P, CH, PIX], f32)
        xn32 = sb("xn32", [P, CH, HR, PADW], f32)
        xw = sb("xw", [P, 2, CH, 2, PAIRS, 2, P], f16)
        xc = sb("xc", [P, CH, 2, K3, P], f16)
        stage = sb("stage", [P, SR * sum(WID[CHUNKS[-1][0]:])], f32)
        res = sb("res", [P, 2, CH, SR, W], f32)
        agg = sb("agg", [P, 2, 2, CH * R, PIX], f16)
        xT = sb("xT", [P, 2, 4 * P], f16)
        band = sb("band", [P, 2, 2, R, SR * TW], f16)
        wT = sb("wT", [KROWS, 2, SR, W], f16)
        proj = sb("proj", [P, 2, CH * R, C], f16)
        idn = sb("idn", [P, P], f16)
        selw = sb("selw", [KROWS, 3, R, 2, P], f16)
        msk = sb("msk", [P, SR * TW], f16)
        msk12 = sb("msk12", [P, SR * WID[-1]], f16)
        gav = sb("gav", [P, P], f32)
        flg = sb("flg", [P, SPI, 2], f32)
        gb = sb("gb", [P, N16], f32)
        bpt = sb("bpt", [P, CH], f32)
        wg32 = sb("wg32", [P, CH, N16], f32)
        wgr = sb("wgr", [P, CH, N16], f32)
        wg3 = sb("wg3", [P, CH, 3, N16], bf16)
        desc = sb("desc", [P, 1], f32)
        pmax = sb("pmax", [P, 2], f32)
        pbits = sb("pbits", [P, 3], i32)
        st6 = sb("st6", [P, CH, 3, 6], f32)
        mv = sb("mv", [P, SPI, CH, 2], f32)
        mvc = sb("mvc", [P, CH, 2], f32)
        gm = sb("gm", [P, CH], f32)
        dev = sb("dev", [P, SPI, CH], f32)
        qv = sb("qv", [P, SPI, CH], f32)
        vr = sb("vr", [P, 4, CH], f32)
        coef = sb("coef", [P, 2, 2, CH], f32)
        cc = sb("cc", [P, 2, CH], f32)
        cf = sb("cf", [P, 2], f32)
        lg = sb("lg", [P, K3, N16], f32)
        mx = sb("mx", [P, K3], f32)
        lm = sb("lm", [P, K3, R], f32)
        az = sb("az", [P, K3, 2 * R], f32)
        sp = sb("sp", [P, K3, 2 * R], f32)
        e4 = sb("e4", [P, K3, R], f32)
        emp = sb("emp", [P, 2, K3, R], f32)
        ab = sb("ab", [P, 4, K3, R], f32)
        th = sb("th", [P, 4, K3, R], f32)
        pol = sb("pol", [P, 2, K3, R], f32)
        uu = sb("uu", [P, K3, 4, R], f32)
        ea = sb("ea", [P, K3, 4, R], f32)
        eb = sb("eb", [P, K3, 4, R], f32)
        zz = sb("zz", [P, 4, K3], f32)
        wf = sb("wf", [P, K3, 5, R], f32)
        w5 = sb("w5", [P, K3, 5, R, 2], f16)
        wcT = sb("wcT", [WROWS, 3, P], f16)
        prm = sb("prm", [WROWS, K3, KROWS], f16)

        psV = pb("psV", [P, 2, 512], f32)
        psA = pb("psA", [P, 2, 512], f32)
        psP = pb("psP", [P, 2, 512], f32)
        psT = pb("psT", [P, 4 * P * 2], f16)
        psG = pb("psG", [P, 512], f32)
        psG16 = psG[:, :].bitcast(f16)

        tmp = agg[:, 1].rearrange("p a k n -> p (a k n)").bitcast(f32)
        wv_s = tmp[:, 0:512].rearrange("p (a c) -> p a c", a=2)
        wp_s = tmp[:, 512:2560].rearrange("p (q c) -> p q c", q=2 * R)
        p32 = tmp[:, 2560:4608].rearrange("p (k c) -> p k c", k=CH * R)
        ptm = tmp[:, 4608:6656].rearrange("p (k c) -> p k c", k=CH * R)

        early = agg[:, 0].rearrange("p a k n -> p (a k n)").bitcast(f32).rearrange(
            "p (c h n) -> p c h n", c=EARLY, h=CH)

        consts_in = sem("consts_in")
        tables_in = sem("tables_in")
        x_in = [sem("x_in0"), sem("x_in1")]
        stat_loaded = [sem("stat_loaded0"), sem("stat_loaded1")]
        early_in = [sem(f"early_in{c}") for c in range(EARLY)]
        stored = [sem("stored0"), sem("stored1")]
        init_done = sem("init_done")
        pT_done = sem("pT_done")
        pT_copied = sem("pT_copied")
        pmax_done = sem("pmax_done")
        wready = sem("wready")
        p_scaled = sem("p_scaled")
        p_split = sem("p_split")
        stats_chain = sem("stats_chain")
        mean_ready = sem("mean_ready")
        gsum_done = sem("gsum_done")
        coef_made = sem("coef_made")
        rstd_ready = sem("rstd_ready")
        ln_done = sem("ln_done")
        coef_chain = sem("coef_chain")
        passed = sem("passed")
        normed = sem("normed")
        edged = sem("edged")
        xc_hi = sem("xc_hi")
        xc_lo = sem("xc_lo")
        xw_hi = sem("xw_hi")
        xw_lo = sem("xw_lo")
        res_ready = sem("res_ready")
        gates_done = sem("gates_done")
        geo = sem("geo")
        act_geo = sem("act_geo")
        kinds_turned = sem("kinds_turned")
        kinds_copied = sem("kinds_copied")
        w_turned = sem("w_turned")
        w_copied = sem("w_copied")
        tile_turned = sem("tile_turned")
        tile_copied = sem("tile_copied")
        picked = sem("picked")
        banded = sem("banded")
        agg_done = sem("agg_done")
        agg_hi = sem("agg_hi")
        agg_lo = sem("agg_lo")
        proj_done = sem("proj_done")
        staged = sem("staged")
        out_added = [sem("out_added0"), sem("out_added1")]

        def windows(h, row):
            v = xn32[:, h, TR * row:TR * row + WIN_R]
            step, size = v.ap[-1][0], v.ap[-2][0]
            return bass.AP(v.tensor, v.offset, [list(v.ap[0]), [TW * step, PAIRS], [size, WIN_R], [step, WIN_W]])

        def rows_by_class(h):
            return xn32[:, h, 1:SR + 1, 1:W + 1].rearrange("p (m k) w -> p k m w", k=3)

        def by_class(v):
            return v.rearrange("p k n -> p (k n)").rearrange("p (k m w) -> p k m w", k=3, w=W)

        def hold(eng):
            eng.sem_inc(passed, 1)

        def wait(eng, s, v):
            if isinstance(v, int) and v <= 0:
                return
            eng.wait_ge(s, v)

        GEO, AGEO, COEF, STAT, FIN, WREADY = 48, 7, 2, 9, 11, 11
        G_LOGITS, G_HYPER, G_EXPONENTS = 6, 14, 38
        FIRST = 1
        STAGED = 2
        NCONST = 6
        NTABLES = 6

        block = ctx.enter_context(nc.Block())

        @block.sync
        def _(sp_):
            def load_x(m, par):
                b = (m & (STRIPS - 1)) // SPI if not isinstance(m, int) else m // SPI
                s, up, down = m & (SPI - 1), (m + SPI - 1) & (SPI - 1), (m + 1) & (SPI - 1)
                sp_.dma_start(xs[:, par, :, 1:SR + 1, :].rearrange("p h r w -> p h (r w)"),
                              at2(xb, b, s)).then_inc(x_in[par], 16)
                for row, t, r in ((0, up, SR - 1), (HR - 1, down, 0)):
                    sp_.dma_start(xs[:, par, :, row, :], at3(xv, b, t, r)).then_inc(x_in[par], 16)

            def at2(v, b, s):
                return v[b, s]

            def at3(v, b, s, r):
                return v[b, s, r]

            def load_stats(k, h):
                b = (k & (STRIPS - 1)) // SPI if not isinstance(k, int) else k // SPI
                if not isinstance(k, int) or k > SPI:
                    wait(sp_, stats_chain, k * STAT - STAT + 3 * h + 3)
                    hold(sp_)
                sp_.dma_start(stat_in[:, h], at2(xb, b, k & (SPI - 1))[:, h]).then_inc(stat_loaded[h], 16)

            def load_strip(n, par):
                wait(sp_, res_ready, n + 1)
                wait(sp_, normed, 2 * n + 2)
                hold(sp_)
                load_x(n + 2, par)

            def step(n, par, load, store, stats=True):
                if load and stats:
                    load_stats(n + AHEAD + 1, 0)
                if load:
                    load_strip(n, par)
                if load and stats:
                    load_stats(n + AHEAD + 1, 1)
                if store:
                    b = (n - 1) // SPI
                    dst, src = at2(ov, b, (n - 1) & (SPI - 1)), res[:, 1 - par].rearrange("p h r w -> p h (r w)")
                    if load or stats:
                        for oh in range(CH):
                            wait(sp_, out_added[oh], len(CHUNKS) * n + FIRST)
                        hold(sp_)
                        sp_.dma_start(dst, src).then_inc(stored[1 - par], 16)
                    else:
                        for oh in range(CH):
                            wait(sp_, out_added[oh], len(CHUNKS) * n + FIRST)
                            hold(sp_)
                            sp_.dma_start(dst[:, oh], src[:, oh]).then_inc(stored[1 - par], 16)

            load_x(0, 0)
            load_x(1, 1)
            for dst, src in (
                (wg32[:], wgT.rearrange("(h p) g -> p h g", p=P)), (gb[:], gbias), (gav[:], gavg), (flg[:], flags),
                (bpt[:], bp), (idn[:], ident),
            ):
                sp_.dma_start(dst, src).then_inc(consts_in, 16)
            for k in range(2, 2 + EARLY):
                sp_.dma_start(early[:, k - 2], at2(xb, 0, k)).then_inc(early_in[k - 2], 16)
            for k in range(2 + EARLY, SPI):
                wait(sp_, stats_chain, (k - EARLY) * STAT + 6)
                hold(sp_)
                sp_.dma_start(early[:, k - 2 - EARLY], at2(xb, 0, k)).then_inc(early_in[k - 2 - EARLY], 16)
            for dst, src in (
                (wv_s, wvT.rearrange("(a p) c -> p a c", p=P)),
                (wp_s, wpT.rearrange("(q p) c -> p q c", p=P)),
                (prm[:], perm), (selw[:], sel), (msk[:], mask), (msk12[:], mask12),
            ):
                sp_.dma_start(dst, src).then_inc(tables_in, 16)
            load_stats(SPI, 0)
            load_stats(SPI, 1)
            for k in range(SPI + 1, AHEAD + 1):
                load_stats(k, 0)
                load_stats(k, 1)
            load_strip(0, 0)
            load_stats(AHEAD + 1, 0)
            load_stats(AHEAD + 1, 1)
            with sp_.Fori(0, (STRIPS - 4) // 2, 1) as d:
                step(d * 2 + 1, 1, True, True)
                step(d * 2 + 2, 0, True, True)
            step(STRIPS - 3, 1, True, True, False)
            step(STRIPS - 2, 0, False, True)
            step(STRIPS - 1, 1, False, True)
            step(STRIPS, 0, False, True, False)
            sp_.wait_ge(stored[0], 16 * STRIPS // 2 + 16)
            sp_.wait_ge(stored[1], 16 * STRIPS // 2 + 32)

        @block.gpsimd
        def _(pool):
            def clear_edges(m):
                wait(pool, normed, 2 * m + 2)
                nc.gpsimd.tensor_tensor(
                    xn32[:, :, 0:HR:HR - 1, 1:W + 1], xn32[:, :, 0:HR:HR - 1, 1:W + 1],
                    cf[:, :].unsqueeze(1).unsqueeze(3).broadcast_to([P, CH, 2, W]), MUL).then_inc(edged, 1)

            def class_lo(m, halves=(0, 1)):
                for h in halves:
                    wait(pool, xc_hi, 2 * m + h + 1)
                    nc.gpsimd.tensor_tensor(by_class(xc[:, h, 1]), rows_by_class(h), by_class(xc[:, h, 0]),
                                            SUB).then_inc(xc_lo, 1)

            def window_lo(m, par, h):
                for row in range(2):
                    wait(pool, xw_hi, 4 * m + 2 * h + row + 1)
                    i = nc.gpsimd.tensor_tensor(xw[:, par, h, 1, :, row], windows(h, row), xw[:, par, h, 0, :, row], SUB)
                i.then_inc(xw_lo, 1)

            def residual(n, par):
                wait(pool, stored[par], 16 * (n // 2) + 16 if isinstance(n, int) else (n - par) * 8 + 16)
                hold(pool)
                for h in range(CH):
                    i = nc.gpsimd.tensor_scalar(res[:, par, h], xs[:, par, h, 1:SR + 1], 1.0, bpt[:, h:h + 1], MUL, ADD)
                i.then_inc(res_ready, 1)

            for oh in range(CH):
                pool.sem_inc(out_added[oh], FIRST)
            for par in range(2):
                pool.sem_inc(stored[par], 16)
            nc.gpsimd.memset(xn32[:].rearrange("p h r w -> p (h r w)"), 0.0).then_inc(init_done, 1)
            pool.wait_ge(consts_in, 16 * NCONST)
            clear_edges(0)
            class_lo(0, (0,))
            window_lo(0, 0, 0)
            window_lo(0, 0, 1)
            clear_edges(1)
            class_lo(1)
            pool.wait_ge(wready, 6)
            nc.gpsimd.partition_all_reduce(pmax[:, 1:2], pmax[:, 0:1], P, bass.bass_isa.ReduceOp.max).then_inc(pmax_done, 1)

            def add_out(n, par, u):
                oh, (a, b) = u % 2, CHUNKS[u // 2]
                pool.wait_ge(staged, n * UNITS + u + 1 + STAGED)
                if u == 0:
                    pool.wait_ge(res_ready, n + 1)
                off = 0
                for c, d in ((a, min(b, PAIRS - 1)), (PAIRS - 1, b)):
                    if c < d:
                        w, k = WID[c], d - c
                        o = res[:, par, oh, :, TW * c:TW * c + k * w].rearrange("p r (j n) -> p j r n", j=k)
                        src = stage[:, off:off + k * SR * w].rearrange("p (j r n) -> p j r n", j=k, r=SR)
                        i = nc.gpsimd.tensor_tensor(o, src, o, ADD)
                        off += k * SR * w
                i.then_inc(out_added[oh], 1)

            def step(n, par, main, more, ahead, before=True):
                for t in range(TILES):
                    if main and t == 1:
                        residual(n, par)
                    if more and t in (3, 5):
                        window_lo(n + 1, 1 - par, (t - 3) // 2)
                    for late, u in units(PDONE[2 * t], before, main):
                        add_out(n - late, 1 - par if late else par, u)
                    if not before and t == 4:
                        pool.wait_ge(p_scaled, 2)
                        nc.gpsimd.tensor_tensor(proj[:, 1], ptm, proj[:, 0], SUB).then_inc(p_split, 1)
                    if ahead and t == 9:
                        clear_edges(n + 2)
                        class_lo(n + 2, (0,))
                    if ahead and t == 12:
                        class_lo(n + 2, (1,))
                    for late, u in units(PDONE[2 * t + 1], before, main):
                        add_out(n - late, 1 - par if late else par, u)

            step(0, 0, True, True, True, before=False)
            with pool.Fori(0, (STRIPS - 4) // 2, 1) as d:
                step(d * 2 + 1, 1, True, True, True)
                step(d * 2 + 2, 0, True, True, True)
            step(STRIPS - 3, 1, True, True, True)
            step(STRIPS - 2, 0, True, True, False)
            step(STRIPS - 1, 1, True, False, False)
            step(STRIPS, 0, False, False, False)

        @block.scalar
        def _(act):
            def normalise(m, par, h):
                if h == 0:
                    wait(act, x_in[par], 48 * (m // 2) + 48 if isinstance(m, int) else (m - par) * 24 + 48)
                    wait(act, coef_chain, COEF * m + COEF)
                wait(act, xw_lo, 2 * m - 1 + h)
                nc.scalar.activation(xn32[:, h, :, 1:W + 1], xs[:, par, h], ACT.Identity, bias=cc[:, 1, h:h + 1],
                                     scale=cc[:, 0, h:h + 1]).then_inc(normed, 1)

            def class_hi(m, h):
                wait(act, edged, m + 1)
                wait(act, gates_done, m)
                nc.scalar.activation(by_class(xc[:, h, 0]), rows_by_class(h), ACT.Copy).then_inc(xc_hi, 1)

            def window_hi(m, par, h, row):
                wait(act, edged, m + 1)
                wait(act, tile_turned, TILES * (m - 1))
                nc.scalar.activation(xw[:, par, h, 0, :, row], windows(h, row), ACT.Copy).then_inc(xw_hi, 1)

            def geo_a(m):
                wait(act, geo, GEO * m + G_LOGITS)
                nc.scalar.activation(e4[:], lm[:], ACT.Exp).then_inc(act_geo, 1)
                nc.scalar.activation(az[:], lg[:, :, 8:16], ACT.Abs).then_inc(act_geo, 1)
                act.wait_ge(act_geo, m * AGEO + 2)
                nc.scalar.activation(az[:], az[:], ACT.Exp, scale=-1.0).then_inc(act_geo, 1)
                act.wait_ge(act_geo, m * AGEO + 3)
                nc.scalar.activation(az[:], az[:], ACT.Ln, bias=1.0).then_inc(act_geo, 1)

            def geo_b(m):
                wait(act, geo, GEO * m + G_HYPER)
                nc.scalar.activation(emp[:, 0], sp[:, :, R:2 * R], ACT.Exp, scale=-2.0).then_inc(act_geo, 1)
                nc.scalar.activation(emp[:, 1], sp[:, :, R:2 * R], ACT.Exp, scale=2.0).then_inc(act_geo, 1)

            def geo_c(m):
                wait(act, geo, GEO * m + G_EXPONENTS)
                nc.scalar.activation(ea[:], ea[:], ACT.Exp).then_inc(act_geo, 1)

            def kinds_copy(m):
                wait(act, kinds_turned, m + 1)
                nc.scalar.activation(wcT[:].rearrange("k c n -> k (c n)"), psG16[0:WROWS, 0:3 * P],
                                     ACT.Copy).then_inc(kinds_copied, 1)

            def w_copy(m, par, ky):
                wait(act, w_turned, 3 * m + ky + 1)
                wait(act, picked, TILES * (m - 1))
                src = psG[0:KROWS, 0:3 * P].rearrange("k (c r w) -> k c r w", c=3, r=SR // 3)
                dst = wT[:, par, ky:SR:3, :].rearrange("k r (w c) -> k c r w", c=3)
                nc.scalar.activation(dst, src, ACT.Copy).then_inc(w_copied, 1)

            def rstd(f):
                wait(act, mean_ready, f * FIN - FIN + 6)
                nc.scalar.activation(vr[:, 1], vr[:, 0], ACT.Ln).then_inc(ln_done, 1)
                act.wait_ge(ln_done, f)
                nc.scalar.activation(vr[:, 2], vr[:, 1], ACT.Exp, scale=-0.5).then_inc(rstd_ready, 1)

            def tile_copy(g, slot):
                wait(act, tile_turned, g + 1)
                wait(act, agg_done, 2 * (g - 1))
                nc.scalar.activation(xT[:, slot], psT[:, 0:4 * P], ACT.Copy).then_inc(tile_copied, 1)

            def agg_round(n, par, t, h):
                j, row = t // 2, t % 2
                w = WID[j]
                off = SR * TW * j + row * TR * w
                wait(act, agg_done, n * (2 * TILES) + 2 * t + h + 1)
                nc.scalar.activation(agg[:, par, 0, R * h:R * h + R, off:off + TR * w],
                                     psA[:, h, 0:R * TR * w].rearrange("p (r n) -> p r n", r=R),
                                     ACT.Copy, scale=1.0 / WS).then_inc(agg_hi, 1)

            def stage_out(n, u):
                oh, (a, b) = u % 2, CHUNKS[u // 2]
                cols = SR * sum(WID[a:b])
                wait(act, proj_done, n * UNITS + u + 1 + FIRST)
                wait(act, out_added[1 - oh], n * len(CHUNKS) + (u + 1) // 2 + FIRST)
                nc.scalar.activation(stage[:, 0:cols], psP[:, oh, 0:cols], ACT.Identity,
                                     scale=desc[:, 0:1]).then_inc(staged, 1)

            act.sem_inc(staged, STAGED)
            nc.scalar.preload_act_table_set("natural_log_exp_and_others")

            def copy_weights(ks):
                for k in ks:
                    act.wait_ge(pT_done, k + 1)
                    nc.scalar.activation(p32[:, k], psA[:, k % 2, 0:C], ACT.Copy).then_inc(pT_copied, 1)

            rstd(1)
            act.wait_ge(init_done, 1)
            for h in range(CH):
                normalise(0, 0, h)
            for h in range(CH):
                class_hi(0, h)
            for h in range(CH):
                for row in range(2):
                    window_hi(0, 0, h, row)
            geo_a(0)
            copy_weights((0, 1, 2, 3))
            geo_b(0)
            copy_weights((4, 5))
            normalise(1, 1, 0)
            copy_weights((6, 7))
            geo_c(0)
            normalise(1, 1, 1)
            tile_copy(0, 0)
            kinds_copy(0)
            for ky in range(3):
                w_copy(0, 0, ky)
            for h in range(CH):
                class_hi(1, h)

            def step(n, par, main, more, ahead, f=None, first=False):
                if main:
                    wait(act, proj_done, n * UNITS - UNITS + FIRST)
                for t in range(TILES):
                    if not main:
                        for late, u in units(PDONE[2 * t] + PDONE[2 * t + 1], True, False):
                            stage_out(n - 1, u)
                        continue
                    if more and t == 11:
                        w_copy(n + 1, 1 - par, 0)
                    agg_round(n, par, t, 0)
                    if more and t == 10:
                        kinds_copy(n + 1)
                    if more and t == 11:
                        w_copy(n + 1, 1 - par, 1)
                    if more or t < TILES - 1:
                        tile_copy(n * TILES + t + 1, (t + 1) % 2)
                    for late, u in units(PDONE[2 * t], not first, True):
                        stage_out(n - late, u)
                    agg_round(n, par, t, 1)
                    if more and t == 11:
                        w_copy(n + 1, 1 - par, 2)
                    for late, u in units(PDONE[2 * t + 1], not first, True):
                        stage_out(n - late, u)
                    if first and t == 1:
                        act.wait_ge(wready, WREADY)
                        nc.scalar.activation(ptm, p32, ACT.Identity,
                                             scale=pbits[:, 1:2].bitcast(f32)).then_inc(p_scaled, 1)
                    if first and t == 2:
                        act.wait_ge(p_scaled, 1)
                        nc.scalar.activation(proj[:, 0], ptm, ACT.Copy).then_inc(p_scaled, 1)
                    if more and t == (2 if first else 0):
                        geo_a(n + 1)
                    if more and t in (1, 2, 3, 4):
                        window_hi(n + 1, 1 - par, (t - 1) // 2, (t - 1) % 2)
                    if more and t == 5:
                        geo_b(n + 1)
                    if f is not None and t == 3:
                        rstd(f)
                    if more and t == 7:
                        geo_c(n + 1)
                    if ahead and t in (7, 8):
                        normalise(n + 2, par, t - 7)
                    if ahead and t in (9, 11):
                        class_hi(n + 2, (t - 9) // 2)

            step(0, 0, True, True, True, first=True)
            with act.Fori(0, (STRIPS - 4) // 2, 1) as d:
                step(d * 2 + 1, 1, True, True, True)
                step(d * 2 + 2, 0, True, True, True, d + 2)
            step(STRIPS - 3, 1, True, True, True)
            step(STRIPS - 2, 0, True, True, False)
            step(STRIPS - 1, 1, True, False, False)
            step(STRIPS, 0, False, False, False)

        @block.vector
        def _(dve):
            class Chain:

                def __init__(self, s, base, n=0):
                    self.s, self.base, self.n = s, base, n
                    if n:
                        dve.wait_ge(s, base + n)

                def link(self, ins, hold=True):
                    self.n += 1
                    ins.then_inc(self.s, 1)
                    if hold:
                        dve.wait_ge(self.s, self.base + self.n)

            def tt(o, a, b, op):
                return nc.vector.tensor_tensor(o, a, b, op)

            def ts(o, a, s1, s2, o1, o2):
                return nc.vector.tensor_scalar(o, a, s1, s2, o1, o2)

            def stt(o, a, s, b, o1, o2):
                return nc.vector.scalar_tensor_tensor(o, a, s, b, o1, o2)

            def statistics(k, i):
                h, c = i // 3, i % 3
                if c == 0:
                    wait(dve, stat_loaded[h], k * 16 - (SPI - 1) * 16)
                    wait(dve, stats_chain, k * STAT)
                nc.vector.bn_stats(st6[:, h, c], stat_in[:, h, c * 384:(c + 1) * 384]).then_inc(stats_chain, 1)

            def early_statistics(k):
                if k < 2:
                    dve.wait_ge(x_in[k], 48)
                else:
                    dve.wait_ge(early_in[(k - 2) % EARLY], 16 + 16 * ((k - 2) // EARLY))
                wait(dve, stats_chain, k * STAT)
                for h in range(CH):
                    src = (xs[:, k, h, 1:SR + 1].rearrange("p r w -> p (r w)") if k < 2
                           else early[:, (k - 2) % EARLY, h])
                    for c in range(3):
                        nc.vector.bn_stats(st6[:, h, c], src[:, c * 384:(c + 1) * 384]).then_inc(stats_chain, 1)

            def chunk_moments(k):
                ch = Chain(stats_chain, k * STAT, 6)
                hold(dve)
                for h in range(CH):
                    ch.link(nc.vector.bn_aggr(mvc[:, h], st6[:, h].rearrange("p c s -> p (c s)")), h == 1)
                ch.link(nc.vector.tensor_copy(mv[:, k & (SPI - 1)], mvc[:]))
                assert ch.n == STAT

            def group_mean(f):
                ch = Chain(mean_ready, f * FIN - FIN)
                dve.wait_ge(gsum_done, f * 2 - 1)
                ch.link(nc.vector.tensor_reduce(gm[:], psG[:, 0:SPI * CH].rearrange("p (k h) -> p h k", h=CH), AX.X, ADD))
                ch.link(tt(dev[:], mv[:, :, :, 0], gm[:].unsqueeze(1).broadcast_to([P, SPI, CH]), SUB))
                ch.link(tt(dev[:], dev[:], dev[:], MUL))
                ch.link(tt(qv[:], dev[:], mv[:, :, :, 1], ADD))

            def group_variance(f):
                ch = Chain(mean_ready, f * FIN - FIN, 4)
                dve.wait_ge(gsum_done, f * 2)
                ch.link(nc.vector.tensor_reduce(vr[:, 3], psG[:, 0:SPI * CH].rearrange("p (k h) -> p h k", h=CH), AX.X, ADD))
                i = ts(vr[:, 0], vr[:, 3], GN_EPS, None, ADD, ALU.bypass)
                ch.link(i)

            def coefficients(f, k):
                ch = Chain(mean_ready, f * FIN - FIN, 6)
                dve.wait_ge(rstd_ready, f)
                slot = (k // SPI) & 1
                ch.link(tt(vr[:, 3], vr[:, 0], vr[:, 2], MUL))
                ch.link(tt(vr[:, 3], vr[:, 3], vr[:, 2], MUL))
                ch.link(ts(vr[:, 3], vr[:, 3], -0.5, 1.5, MUL, ADD))
                ch.link(stt(vr[:, 3], vr[:, 2], XS, vr[:, 3], MUL, MUL))
                ch.link(nc.vector.tensor_copy(coef[:, slot, 0], vr[:, 3]), False)
                stt(coef[:, slot, 1], gm[:], -1.0, vr[:, 3], MUL, MUL).then_inc(coef_made, 1)
                dve.wait_ge(coef_made, f)
                assert ch.n == FIN

            def strip_coefficients(m):
                wait(dve, edged, m)
                slot = ((m // SPI) & 1)
                nc.vector.tensor_copy(cc[:], coef[:, slot]).then_inc(coef_chain, 1)
                nc.vector.tensor_copy(cf[:], flg[:, m & (SPI - 1)]).then_inc(coef_chain, 1)

            def b16(a):
                return a.unsqueeze(2).broadcast_to([P, K3, 4, R])

            r_, k_, r2_, s_, c_ = th[:, 0], th[:, 1], th[:, 2], pol[:, 0], pol[:, 1]

            def series(ch, q):
                ch.link(stt(s_, s_, SIN[q], r2_, ADD, MUL), False)
                ch.link(stt(c_, c_, COS[q], r2_, ADD, MUL), False)

            def geometry(m, part):
                if part == 0:
                    ch = Chain(geo, m * GEO)
                    dve.wait_ge(gates_done, m + 1)
                    ch.link(nc.vector.tensor_reduce(
                        lg[:], psG[:, 0:K3 * 48].rearrange("p (k t c) -> p k c t", k=K3, t=3), AX.X, ADD))
                    ch.link(stt(lg[:], lg[:], 1.0 / XS, gb[:].unsqueeze(1).broadcast_to([P, K3, N16]), MUL, ADD), False)
                elif part == 1:
                    ch = Chain(geo, m * GEO, 2)
                    ch.link(nc.vector.tensor_reduce(mx[:], lg[:, :, 0:R], AX.X, MAX), False)
                    ch.link(ts(k_, lg[:, :, R:2 * R], 1.0 / np.pi, ROUND, MUL, ADD))
                    ch.link(tt(lm[:], lg[:, :, 0:R], mx[:].unsqueeze(2).broadcast_to([P, K3, R]), SUB), False)
                    ch.link(ts(k_, k_, ROUND, None, SUB, ALU.bypass), False)
                    assert ch.n == G_LOGITS
                elif part == 2:
                    ch = Chain(geo, m * GEO, 6)
                    ch.link(stt(r_, k_, -PI_PARTS[0], lg[:, :, R:2 * R], MUL, ADD))
                    ch.link(stt(r_, k_, -PI_PARTS[1], r_, MUL, ADD))
                    ch.link(stt(r_, k_, -PI_PARTS[2], r_, MUL, ADD), False)
                elif part == 3:
                    ch = Chain(geo, m * GEO, 9)
                    ch.link(tt(r2_, r_, r_, MUL), False)
                    dve.wait_ge(act_geo, m * AGEO + 4)
                    ch.link(stt(sp[:], lg[:, :, 8:16], 0.0, az[:], MAX, ADD))
                    ch.link(ts(s_, r2_, SIN[-1], None, MUL, ALU.bypass), False)
                    ch.link(ts(c_, r2_, COS[-1], None, MUL, ALU.bypass), False)
                    ch.link(ts(sp[:, :, R:2 * R], sp[:, :, R:2 * R], MIN_HYP, MAX_HYP, MAX, MIN), False)
                    assert ch.n == G_HYPER
                elif part == 4:
                    ch = Chain(geo, m * GEO, 14)
                    series(ch, 4)
                    ch.link(ts(ab[:, 2], sp[:, :, 0:R], BASE_EPS, None, ADD, ALU.bypass))
                    series(ch, 3)
                    ch.link(tt(ab[:, 2], ab[:, 2], ab[:, 2], MUL), False)
                elif part == 5:
                    ch = Chain(geo, m * GEO, 20)
                    series(ch, 2)
                    ch.link(nc.vector.reciprocal(ab[:, 2], ab[:, 2]))
                    series(ch, 1)
                elif part == 6:
                    ch = Chain(geo, m * GEO, 25)
                    series(ch, 0)
                    dve.wait_ge(geo, m * GEO + 27)
                    ch.link(stt(uu[:, :, 2], s_, 1.0, r_, ADD, MUL), False)
                    ch.link(ts(uu[:, :, 0], c_, 1.0, None, ADD, ALU.bypass), False)
                elif part == 7:
                    ch = Chain(geo, m * GEO, 29)
                    ch.link(tt(uu[:, :, 1], uu[:, :, 0], uu[:, :, 2], ADD), False)
                    ch.link(tt(uu[:, :, 3], uu[:, :, 0], uu[:, :, 2], SUB), False)
                    dve.wait_ge(act_geo, m * AGEO + 6)
                    ch.link(stt(ab[:, 0], emp[:, 0], -0.5, ab[:, 2], MUL, MUL), False)
                    ch.link(stt(ab[:, 1], emp[:, 1], -0.5, ab[:, 2], MUL, MUL))
                    ch.link(tt(uu[:], uu[:], uu[:], MUL), False)
                elif part == 8:
                    ch = Chain(geo, m * GEO, 34)
                    ch.link(tt(ea[:], uu[:], b16(ab[:, 0]), MUL), False)
                    bb = ab[:, 1].unsqueeze(2).broadcast_to([P, K3, 2, R])
                    ch.link(tt(eb[:, :, 0:2], uu[:, :, 2:4], bb, MUL), False)
                    ch.link(tt(eb[:, :, 2:4], uu[:, :, 0:2], bb, MUL))
                    ch.link(tt(ea[:], ea[:], eb[:], ADD), False)
                    assert ch.n == G_EXPONENTS
                elif part == 9:
                    ch = Chain(geo, m * GEO, 38)
                    dve.wait_ge(act_geo, m * AGEO + 7)
                    ch.link(tt(eb[:], ea[:], b16(e4[:]), MUL), False)
                    ch.link(nc.vector.tensor_reduce(zz[:, 1], e4[:], AX.X, ADD))
                    ch.link(nc.vector.tensor_reduce(zz[:, 0], eb[:].rearrange("p k j r -> p k (j r)"), AX.X, ADD))
                    ch.link(stt(zz[:, 0], zz[:, 0], 2.0, zz[:, 1], MUL, ADD), False)
                elif part == 10:
                    ch = Chain(geo, m * GEO, 42)
                    ch.link(stt(zz[:, 0], zz[:, 1], SUM_EPS, zz[:, 0], MUL, ADD))
                    ch.link(nc.vector.reciprocal(zz[:, 2], zz[:, 0]))
                    rz = zz[:, 2].unsqueeze(2)
                    ch.link(stt(wf[:, :, 0:4].rearrange("p k j r -> p k (j r)"), eb[:].rearrange("p k j r -> p k (j r)"),
                                WS, rz.broadcast_to([P, K3, 4 * R]), MUL, MUL), False)
                    ch.link(stt(wf[:, :, 4], e4[:], WS, rz.broadcast_to([P, K3, R]), MUL, MUL))
                    wait(dve, kinds_turned, m)
                    f = wf[:].rearrange("p k j r -> p k (j r)")
                    hi = w5[:, :, :, :, 0].rearrange("p k j r -> p k (j r)")
                    lo = w5[:, :, :, :, 1].rearrange("p k j r -> p k (j r)")
                    ch.link(nc.vector.tensor_copy(hi, f))
                    ch.link(tt(lo, f, hi, SUB), False)
                    assert ch.n == GEO

            def band_mask(n, par, t, v):
                p, part = t // 2, t % 2
                slot, w = (par + p) % 2, WID[p]
                dve.wait_ge(picked, v + 1)
                m = msk[:] if w == TW else msk12[:]
                wait(dve, agg_done, 2 * (v - 2) if part == 0 else 0)
                src = psV[:, :, 0:2 * SR * w].rearrange("p b (r n) -> p b r n", r=2)
                tt(band[:, slot, part, :, 0:SR * w].rearrange("p (b r) n -> p b r n", b=2), src,
                   m.unsqueeze(1).unsqueeze(1).broadcast_to([P, 2, 2, SR * w]), MUL).then_inc(banded, 1)

            def agg_rest(n, par, t, h):
                j, row = t // 2, t % 2
                w = WID[j]
                off = SR * TW * j + row * TR * w
                dve.wait_ge(agg_hi, n * (2 * TILES) + 2 * t + h + 1)
                stt(agg[:, par, 1, R * h:R * h + R, off:off + TR * w],
                    psA[:, h, 0:R * TR * w].rearrange("p (r n) -> p r n", r=R), 1.0 / WS,
                    agg[:, par, 0, R * h:R * h + R, off:off + TR * w], MUL, SUB).then_inc(agg_lo, 1)

            def prepare_gates():
                ch = Chain(wready, 0)
                ch.link(nc.vector.tensor_copy(wg3[:, :, 0], wg32[:]))
                ch.link(tt(wgr[:], wg32[:], wg3[:, :, 0], SUB))
                ch.link(nc.vector.tensor_copy(wg3[:, :, 1], wgr[:]))
                ch.link(tt(wgr[:], wgr[:], wg3[:, :, 1], SUB))
                ch.link(nc.vector.tensor_copy(wg3[:, :, 2], wgr[:]), False)

            def largest_weight():
                ch = Chain(wready, 0, 5)
                dve.wait_ge(pT_copied, CH * R)
                ch.link(nc.vector.tensor_reduce(pmax[:, 0:1], p32.rearrange("p k c -> p (k c)"), AX.X, MAX,
                                                apply_absolute_value=True), False)

            def prepare_weights():
                ch = Chain(wready, 0, 6)
                dve.wait_ge(pmax_done, 1)
                ch.link(ts(pmax[:, 1:2], pmax[:, 1:2], 2.0 ** -100, None, MAX, ALU.bypass))
                ch.link(ts(pbits[:, 0:1], pmax[:, 1:2].bitcast(i32), 0x7F800000, None, ALU.bitwise_and, ALU.bypass))
                ch.link(ts(pbits[:, 1:2], pbits[:, 0:1], -1.0, float(267 << 23), MUL, ADD), False)
                ch.link(ts(pbits[:, 2:3], pbits[:, 0:1], 1.0, float(20 << 23), MUL, SUB))
                ch.link(nc.vector.tensor_copy(desc[:], pbits[:, 2:3].bitcast(f32)), False)
                assert ch.n == WREADY

            for k in range(SPI):
                early_statistics(k)
                chunk_moments(k)
                if k == 1:
                    dve.wait_ge(consts_in, 16 * NCONST)
                    prepare_gates()
            group_mean(1)
            group_variance(1)
            coefficients(1, 0)
            strip_coefficients(0)
            for i in range(3 * CH):
                statistics(SPI, i)
            chunk_moments(SPI)
            dve.wait_ge(xc_hi, 2)
            tt(by_class(xc[:, 1, 1]), rows_by_class(1), by_class(xc[:, 1, 0]), SUB).then_inc(xc_lo, 1)
            strip_coefficients(1)
            for part in range(11):
                geometry(0, part)
            largest_weight()
            for i in range(3 * CH):
                statistics(AHEAD - 1, i)
            chunk_moments(AHEAD - 1)
            dve.wait_ge(tables_in, 16 * NTABLES)
            for t in range(2):
                band_mask(0, 0, t, t)

            def step(n, par, main, more, ahead, f=None, before=True, stats=True):
                parts = [(t + 1,) if t < 10 else () for t in range(TILES)]
                if not before:
                    parts[:8] = [(), (), (0, 1), (2,), (3, 4), (5,), (6, 7), (8,)]

                for t in range(TILES):
                    if main and (more or t < TILES - 2):
                        last = t >= TILES - 2
                        band_mask(n, (1 - par) if last else par, t + 2 - (TILES if last else 0), n * TILES + t + 2)
                    if main:
                        agg_rest(n, par, t, 0)
                    if more:
                        for part in parts[t]:
                            geometry(n + 1, part)
                    if f is not None:
                        if t == 1:
                            group_mean(f)
                        if t == 3:
                            group_variance(f)
                        if t == 5:
                            coefficients(f, n + SPI + 1)
                    if not before and t == 0:
                        prepare_weights()
                    if not before and t < 3:
                        for i in range(2):
                            statistics(AHEAD, 2 * t + i)
                    if before and ahead and t in (0, 3):
                        statistics(n + AHEAD, 4 + t // 3)
                    if ahead and t == 7:
                        chunk_moments(n + AHEAD)
                    if ahead and stats and t in (10, 12):
                        for i in range(2):
                            statistics(n + AHEAD + 1, t - 10 + i)
                    if ahead and t == 6:
                        strip_coefficients(n + 2)
                    if main:
                        agg_rest(n, par, t, 1)
                    if ahead and t == TILES - 1:
                        geometry(n + 2, 0)

            step(0, 0, True, True, True, before=False)
            with dve.Fori(0, (STRIPS - 4) // 2, 1) as d:
                step(d * 2 + 1, 1, True, True, True)
                step(d * 2 + 2, 0, True, True, True, d + 2)
            step(STRIPS - 3, 1, True, True, True, stats=False)
            step(STRIPS - 2, 0, True, True, False)
            step(STRIPS - 1, 1, True, False, False)

        @block.tensor
        def _(pe):
            mm = nc.tensor.matmul

            def turn_tile(n, par, t, g):
                if t == 0:
                    wait(pe, xw_lo, 2 * n + 2)
                wait(pe, tile_copied, g)
                for part in range(2):
                    for h in range(CH):
                        q = part * 2 + h
                        i = nc.tensor.transpose(psT[:, q * P:(q + 1) * P],
                                                xw[:, par, h, part, t // 2, t % 2], idn[:])
                i.then_inc(tile_turned, 1)

            def pick(n, par, t, v):
                p, part = t // 2, t % 2
                w, phase = WID[p], (TW * p) % 3
                if t == 0:
                    wait(pe, w_copied, 3 * n + 3)
                wait(pe, banded, v)
                rhs = wT[:, par, :, TW * p:TW * p + w]
                for r in range(R):
                    i = mm(psV[:, r // 2, (r % 2) * SR * w:(r % 2 + 1) * SR * w], selw[:, phase, r, part], rhs,
                           start=True, stop=True)
                i.then_inc(picked, 1)

            def aggregate(n, par, t, h):
                j, row = t // 2, t % 2
                w = WID[j]
                slot = (par + j) % 2
                if h == 0:
                    wait(pe, tile_copied, n * TILES + t + 1)
                    if row == 0:
                        wait(pe, banded, n * TILES + t + 2)
                wait(pe, agg_lo, n * (2 * TILES) + 2 * t + h - 1)
                for q, (xp, bpart) in enumerate(((0, 0), (0, 1), (1, 0))):
                    i = mm(psA[:, h, 0:R * TR * w].rearrange("p (r n) -> p r n", r=R),
                           xT[:, t % 2, (xp * 2 + h) * P:(xp * 2 + h + 1) * P],
                           band[:, slot, bpart, :, row * TR * w:(row + 1) * TR * w], start=q == 0, stop=q == 2)
                i.then_inc(agg_done, 1)

            def project(n, par, idx):
                u, k = idx // PMM, idx % PMM
                oh, (a, b) = u % 2, CHUNKS[u // 2]
                o0, cols = SR * TW * a, SR * sum(WID[a:b])
                if k == 0:
                    if oh == 0:
                        wait(pe, agg_lo, n * (2 * TILES) + 4 * b)
                    wait(pe, staged, n * UNITS + u - 1 + STAGED)
                kk, q = k // 3, k % 3
                pp, ap = ((0, 0), (0, 1), (1, 0))[q]
                i = mm(psP[:, oh, 0:cols], proj[:, pp, kk, oh * P:(oh + 1) * P], agg[:, par, ap, kk, o0:o0 + cols],
                       start=k == 0, stop=k == PMM - 1)
                if k == PMM - 1:
                    i.then_inc(proj_done, 1)

            def gates(m, par):
                wait(pe, xc_lo, 2 * m + 2)
                wait(pe, w_copied, 3 * m)
                for ky in range(3):
                    for kx in range(3):
                        o = psG[:, (ky * 3 + kx) * 48:(ky * 3 + kx + 1) * 48]
                        for q in range(4):
                            part, h = q // 2, q % 2
                            rows = xc[:, h, part].rearrange("p k n -> p (k n)")
                            px = rows[:, ky * 3 * P + kx:(ky + 1) * 3 * P:3]
                            i = mm(o, px, wg3[:, h].rearrange("p t g -> p (t g)"), start=q == 0, stop=q == 3)
                i.then_inc(gates_done, 1)

            def turn_kinds(m):
                wait(pe, geo, GEO * m + GEO)
                for ky in range(3):
                    i = nc.tensor.transpose(psG16[0:WROWS, ky * P:(ky + 1) * P],
                                            w5[:, 3 * ky:3 * ky + 3].rearrange("p k j r t -> p (k j r t)"), idn[:])
                i.then_inc(kinds_turned, 1)

            def turn_weights(m, ky):
                if ky == 0:
                    wait(pe, kinds_copied, m + 1)
                else:
                    wait(pe, w_copied, 3 * m + ky)
                for kx in range(3):
                    i = mm(psG[0:KROWS, kx * P:(kx + 1) * P], prm[:, 3 * ky + kx], wcT[:, ky], start=True, stop=True)
                i.then_inc(w_turned, 1)

            def group_sum(f, which, src):
                i = mm(psG[:, 0:SPI * CH], gav[:], src, start=True, stop=True)
                i.then_inc(gsum_done, 1)

            pe.sem_inc(proj_done, FIRST)
            means = mv[:, :, :, 0]
            pe.wait_ge(consts_in, 16 * NCONST)
            pe.wait_ge(stats_chain, SPI * STAT)
            group_sum(1, 0, means)
            pe.wait_ge(mean_ready, 4)
            group_sum(1, 1, qv[:])
            pe.wait_ge(wready, 5)
            pe.wait_ge(mean_ready, 6)
            gates(0, 0)
            pe.wait_ge(tables_in, 16 * NTABLES)
            for k in range(CH * R):
                h, r = k // R, k % R
                wait(pe, pT_copied, k - 1)
                for a in range(2):
                    i = mm(psA[:, k % 2, 0:C], wv_s[:, a, h * P:(h + 1) * P], wp_s[:, 2 * r + a], start=a == 0, stop=a == 1)
                i.then_inc(pT_done, 1)
            turn_tile(0, 0, 0, 0)
            turn_kinds(0)
            for ky in range(3):
                turn_weights(0, ky)
            for t in range(3):
                pick(0, 0, t, t)

            def step(n, par, main, more, ahead, f=None, before=True):
                for t in range(TILES):
                    if main:
                        aggregate(n, par, t, 0)
                    if more and t == 11:
                        turn_weights(n + 1, 1)
                    for late, idx in units(PSLOTS[2 * t], before, main):
                        project(n - late, 1 - par if late else par, idx)
                    if more and t == 10:
                        if f is not None:
                            pe.wait_ge(mean_ready, f * FIN - FIN + 6)
                        turn_kinds(n + 1)
                    if main and (more or t < TILES - 1):
                        last = t == TILES - 1
                        turn_tile(n + 1 if last else n, 1 - par if last else par, 0 if last else t + 1, n * TILES + t + 1)
                    if not before and t == 1:
                        gates(1, 1)
                    if not before and t == 5:
                        pe.wait_ge(p_split, 1)
                    if ahead and t == 13:
                        gates(n + 2, par)
                    if main:
                        aggregate(n, par, t, 1)
                    if more and t == 11:
                        turn_weights(n + 1, 2)
                    for late, idx in units(PSLOTS[2 * t + 1], before, main):
                        project(n - late, 1 - par if late else par, idx)
                    if f is not None and t == 0:
                        wait(pe, stats_chain, (n + AHEAD) * STAT)
                        wait(pe, geo, n * GEO + GEO + 1)
                        group_sum(f, 0, means)
                    if f is not None and t == 2:
                        pe.wait_ge(mean_ready, f * FIN - FIN + 4)
                        group_sum(f, 1, qv[:])
                    if more and t == 10:
                        turn_weights(n + 1, 0)
                    if main and (more or t < TILES - 3):
                        last = t >= TILES - 3
                        pick(n + 1 if last else n, 1 - par if last else par, t + 3 - (TILES if last else 0), n * TILES + t + 3)

            step(0, 0, True, True, True, before=False)
            with pe.Fori(0, (STRIPS - 4) // 2, 1) as d:
                step(d * 2 + 1, 1, True, True, True)
                step(d * 2 + 2, 0, True, True, True, d + 2)
            step(STRIPS - 3, 1, True, True, True)
            step(STRIPS - 2, 0, True, True, False)
            step(STRIPS - 1, 1, True, False, False)
            step(STRIPS, 0, False, False, False)


def shape_tables():
    win = np.arange(P)
    wy, wx = win // WIN_W - 1, win % WIN_W - 1
    sel = np.zeros((K3, R, 2, 3, R, 2, P), np.float16)
    for phase in range(3):
        cls = ((wy % 3) * 3 + (wx + phase) % 3)
        for r in range(R):
            for part in range(2):
                sel[cls, r, part, phase, r, part, win] = 1.0
    sel = sel.reshape(KROWS, 3, R, 2, P)

    kind = {(0, 1): 0, (0, -1): 0, (1, 1): 1, (-1, -1): 1, (1, 0): 2, (-1, 0): 2, (1, -1): 3, (-1, 1): 3, (0, 0): 4}
    perm = np.zeros((3, KINDS, R, 2, K3, K3, R, 2), np.float16)
    for c in range(K3):
        for a in range(K3):
            dy, dx = [(a // 3 - c // 3 + 1) % 3 - 1, (a % 3 - c % 3 + 1) % 3 - 1]
            for r in range(R):
                for part in range(2):
                    perm[c % 3, kind[dy, dx], r, part, c, a, r, part] = 1.0
    perm = perm.reshape(WROWS, K3, KROWS)

    def mask(w):
        y, x = np.divmod(np.arange(SR * w), w)
        near = (abs(wy[:, None] - y % TR) <= 1) & (abs(wx[:, None] - x) <= 1)
        return near.astype(np.float16)

    group = np.arange(P) // GROUP
    gavg = (group[:, None] == group).astype(np.float32) / (GROUP * SPI)
    flags = np.ones((P, SPI, 2), np.float32)
    flags[:, 0, 0] = 0.0
    flags[:, SPI - 1, 1] = 0.0
    return {"ident": np.eye(P, dtype=np.float16), "sel": sel, "perm": perm, "mask": mask(TW), "mask12": mask(WID[-1]),
            "gavg": gavg, "flags": flags}


def kernel(x, L0_conv_Wv, L0_conv_Wg, L0_conv_bg, L0_conv_Wgeom, L0_conv_bgeom, L0_conv_Wp, L0_conv_bp):
    import concourse.bacc as bacc
    from concourse.bass_utils import run_bass_kernel_spmd

    arrays = {
        "x": np.ascontiguousarray(x),
        "wv": np.ascontiguousarray(L0_conv_Wv),
        "wpT": np.ascontiguousarray(np.asarray(L0_conv_Wp).T),
        "wgT": np.ascontiguousarray(np.concatenate([np.asarray(L0_conv_Wg), np.asarray(L0_conv_Wgeom)]).T),
        "gbias": np.ascontiguousarray(np.broadcast_to(
            np.concatenate([np.asarray(L0_conv_bg), np.asarray(L0_conv_bgeom)]), (P, N16))),
        "bp": np.ascontiguousarray(np.asarray(L0_conv_bp).reshape(CH, P).T),
        **shape_tables(),
    }
    nc = bacc.Bacc("TRN2", target_bir_lowering=False, num_devices=1)
    args = [nc.dram_tensor(f"in_{n}", a.shape, mybir.dt.from_np(a.dtype), kind="ExternalInput").ap()
            for n, a in arrays.items()]
    out = nc.dram_tensor("out", (B, C, H, W), mybir.dt.float32, kind="ExternalOutput").ap()
    steered_conv(nc, *args, out)
    r = run_bass_kernel_spmd(nc, [{f"in_{n}": a for n, a in arrays.items()}], core_ids=[0])
    return r.results[0]["out"]
```
